# Optimizing a Trainium2 kernel written in Bass

```python
import numpy as np
import jax
import jax.numpy as jnp

def _softmax(x, axis=-1):
    return jax.nn.softmax(x, axis=axis)

def _gelu(x):
    return jax.nn.gelu(x, approximate=True)

def _silu(x):
    return jax.nn.silu(x)

def _sigmoid(x):
    return jax.nn.sigmoid(x)

def _layernorm(x, axis=-1, eps=1e-05):
    m = jnp.mean(x, axis=axis, keepdims=True)
    v = jnp.var(x, axis=axis, keepdims=True)
    return (x - m) / jnp.sqrt(v + eps)

def _scatter_add(tgt, idx, src, axis=0):
    return tgt.at[idx].add(src)

def _segment_sum(src, seg, n):
    return jax.ops.segment_sum(src, seg, n)
kernel_name = 'mk_macaron_d1_jaxref_r8_c379bd'

def setup_inputs(seed: int=0):
    np.random.seed(seed)
    _w = jnp.asarray

    def _L0_attn_setup():
        import jax, jax.numpy as jnp
        import numpy as np
        import math
        DIM = 128
        NUM_HEADS = 16
        HEAD_DIM = DIM // NUM_HEADS
        MAX_BIAS = 8.0
        SCALE = HEAD_DIM ** (-0.5)

        def _alibi_slopes(n):

            def pow2(n):
                start = 2.0 ** (-2.0 ** (-(math.log2(n) - 3)))
                return [start * start ** i for i in range(n)]
            if math.log2(n).is_integer():
                return pow2(n)
            c = 2 ** math.floor(math.log2(n))
            return pow2(c) + _alibi_slopes(2 * c)[0::2][:n - c]

        def _rotate_half(t):
            t1, t2 = jnp.split(t, 2, axis=-1)
            return jnp.concatenate([-t2, t1], axis=-1)
        key = jax.random.key(seed)
        k1, k2, k3, k4 = jax.random.split(key, 4)
        B, N, C = (2, 256, DIM)
        x = jax.random.normal(k1, (B, N, C), dtype=jnp.float32)
        qkv_w = jax.random.normal(k2, (3 * C, C), dtype=jnp.float32) * C ** (-0.5)
        proj_w = jax.random.normal(k3, (C, C), dtype=jnp.float32) * C ** (-0.5)
        proj_b = jax.random.normal(k4, (C,), dtype=jnp.float32) * 0.01
        slopes = jnp.asarray(np.array(_alibi_slopes(NUM_HEADS), dtype=np.float32))
        return {'x': x, 'qkv_w': qkv_w, 'proj_w': proj_w, 'proj_b': proj_b, 'slopes': slopes}
    _L0_attn_in = _L0_attn_setup()

    def _L0_ffn_setup():
        import jax, jax.numpy as jnp
        import numpy as np
        D = 128
        F = 352
        E = 8
        TOP_K = 2
        key = jax.random.key(seed)
        ks = jax.random.split(key, 6)
        std = 0.02
        x = jax.random.normal(ks[0], (2, 256, D), dtype=jnp.float32)
        router_w = jax.random.normal(ks[1], (D, E), dtype=jnp.float32) * std
        w1 = jax.random.normal(ks[2], (E, D, F), dtype=jnp.float32) * std
        v1 = jax.random.normal(ks[3], (E, D, F), dtype=jnp.float32) * std
        w2 = jax.random.normal(ks[4], (E, F, D), dtype=jnp.float32) * std
        bias = jnp.zeros((D,), dtype=jnp.float32)
        return {'x': x, 'router_w': router_w, 'w1': w1, 'v1': v1, 'w2': w2, 'bias': bias}
    _L0_ffn_in = _L0_ffn_setup()
    _d = {'L0_attn_x': _L0_attn_in['x'], 'L0_attn_qkv_w': _L0_attn_in['qkv_w'], 'L0_attn_proj_w': _L0_attn_in['proj_w'], 'L0_attn_proj_b': _L0_attn_in['proj_b'], 'L0_attn_slopes': _L0_attn_in['slopes'], 'L0_ffn_router_w': _L0_ffn_in['router_w'], 'L0_ffn_w1': _L0_ffn_in['w1'], 'L0_ffn_v1': _L0_ffn_in['v1'], 'L0_ffn_w2': _L0_ffn_in['w2'], 'L0_ffn_bias': _L0_ffn_in['bias']}
    _x0 = _d['L0_attn_x']
    _d['L0_attn_x'] = jax.random.normal(jax.random.fold_in(jax.random.key(seed), 1), (8, 256, 128), dtype=_x0.dtype)
    del _x0
    return _d

def reference(L0_attn_x, L0_attn_qkv_w, L0_attn_proj_w, L0_attn_proj_b, L0_attn_slopes, L0_ffn_router_w, L0_ffn_w1, L0_ffn_v1, L0_ffn_w2, L0_ffn_bias):

    def _L0_attn_ref(x, qkv_w, proj_w, proj_b, slopes):
        import jax, jax.numpy as jnp
        import numpy as np
        import math
        DIM = 128
        NUM_HEADS = 16
        HEAD_DIM = DIM // NUM_HEADS
        MAX_BIAS = 8.0
        SCALE = HEAD_DIM ** (-0.5)

        def _alibi_slopes(n):

            def pow2(n):
                start = 2.0 ** (-2.0 ** (-(math.log2(n) - 3)))
                return [start * start ** i for i in range(n)]
            if math.log2(n).is_integer():
                return pow2(n)
            c = 2 ** math.floor(math.log2(n))
            return pow2(c) + _alibi_slopes(2 * c)[0::2][:n - c]

        def _rotate_half(t):
            t1, t2 = jnp.split(t, 2, axis=-1)
            return jnp.concatenate([-t2, t1], axis=-1)
        B, N, C = x.shape
        H, D = (NUM_HEADS, HEAD_DIM)
        qkv = (x @ qkv_w.T).reshape(B, N, 3, H, D).transpose(2, 0, 3, 1, 4)
        q, k, v = (qkv[0], qkv[1], qkv[2])
        inv_freq = 1.0 / 10000.0 ** (jnp.arange(0, D, 2, dtype=jnp.float32) / D)
        freqs = jnp.arange(N, dtype=jnp.float32)[:, None] * inv_freq[None, :]
        sin = jnp.tile(jnp.sin(freqs), (1, 2))
        cos = jnp.tile(jnp.cos(freqs), (1, 2))
        q = q * cos + _rotate_half(q) * sin
        k = k * cos + _rotate_half(k) * sin
        attn = jnp.einsum('bhqd,bhkd->bhqk', q, k) * SCALE
        pos = jnp.arange(N, dtype=jnp.float32)
        diff = pos[None, :] - pos[:, None]
        diff = jnp.where(diff > 0, 0.0, diff)
        alibi = diff[None, :, :] * slopes[:, None, None] * MAX_BIAS
        attn = attn + alibi[None]
        w = jax.nn.softmax(attn, axis=-1)
        out = jnp.einsum('bhqk,bhkd->bhqd', w, v)
        out = out.transpose(0, 2, 1, 3).reshape(B, N, C)
        return out @ proj_w.T + proj_b

    def _L0_ffn_ref(x, router_w, w1, v1, w2, bias):
        import jax, jax.numpy as jnp
        import numpy as np
        D = 128
        F = 352
        E = 8
        TOP_K = 2
        B, S, d = x.shape
        xt = x.reshape(B * S, d)
        scores = jax.nn.softmax(xt @ router_w, axis=-1)
        expert_weights, expert_idx = jax.lax.top_k(scores, TOP_K)
        h = jax.nn.gelu(jnp.einsum('td,edf->tef', xt, w1), approximate=False) * jnp.einsum('td,edf->tef', xt, v1)
        y = jnp.einsum('tef,efd->ted', h, w2)
        yk = jnp.take_along_axis(y, expert_idx[:, :, None], axis=1)
        out = jnp.sum(expert_weights[:, :, None] * yk, axis=1) + bias
        return out.reshape(B, S, d)
    x = L0_attn_x
    x = x + 0.5 * _L0_ffn_ref(_layernorm(x, axis=-1), L0_ffn_router_w, L0_ffn_w1, L0_ffn_v1, L0_ffn_w2, L0_ffn_bias)
    x = x + _L0_attn_ref(_layernorm(x, axis=-1), L0_attn_qkv_w, L0_attn_proj_w, L0_attn_proj_b, L0_attn_slopes)
    x = x + 0.5 * _L0_ffn_ref(_layernorm(x, axis=-1), L0_ffn_router_w, L0_ffn_w1, L0_ffn_v1, L0_ffn_w2, L0_ffn_bias)
    return x

_drawn_inputs = setup_inputs


def setup_inputs(seed=0):
    import zlib

    import numpy as np

    out = dict(_drawn_inputs(seed))
    spreads = {'L0_ffn_bias': (0.0, 0.1)}
    factors = {'L0_attn_proj_b': 5.756,
     'L0_ffn_router_w': 8.0,
     'L0_ffn_w1': 8.0,
     'L0_ffn_v1': 8.0,
     'L0_ffn_w2': 8.0}
    for name, (base, spread) in spreads.items():
        noise = np.random.default_rng([zlib.crc32(name.encode()), seed]).standard_normal(out[name].shape)
        drawn = base * np.exp(spread * noise) if base else spread * noise
        out[name] = jnp.asarray(drawn.astype(out[name].dtype))
    for name, factor in factors.items():
        out[name] = (out[name] * factor).astype(out[name].dtype)
    return out
```

```python
from contextlib import ExitStack

import concourse.bass as bass
from concourse import mybir

F32 = mybir.dt.float32
F32R = mybir.dt.float32r
BF16 = mybir.dt.bfloat16
U32 = mybir.dt.uint32
ALU = mybir.AluOpType
ACT = mybir.ActivationFunctionType
AX = mybir.AxisListType

B, N, D = 8, 256, 128
P = 128
TB = N // P
H, HD = 16, 8
E, F = 8, 352
UNITS = E * TB
FT = E * F
CH = FT // P
STEPS = CH // 2
EPS = 1e-5
VW = 32
PAIRS = [(0, 0), (1, 0), (2, 0), (0, 1), (1, 1), (0, 2)]
QK_ROWS = len(PAIRS) * HD
S_ROWS = QK_ROWS + 6
E_ROWS = S_ROWS + 2
ROUTE = 10
P1A = 8
M_AT, LN_AT, PV_AT, O_AT = 11, 3, 9, 12
XT_AT, V_AT, QK_AT = 4, 6, 7


CQ, CK, CQR, CKR, CV, CP, CR, CEND = 0, 128, 256, 384, 512, 640, 768, 776


def macaron(nc, x, small_w, w1, v1, w2, ffn_bias, proj_b, slopes, ident, dist, dist_t, rope, expert_ids,
            far, ones_rows, out):
    ctx = ExitStack()
    with ctx:
        ctx.enter_context(nc.allow_low_precision(reason="exact splits"))

        def sb(name, shape, dt=F32):
            return ctx.enter_context(nc.sbuf_tensor(name, shape, dt))

        def sem(name):
            return ctx.enter_context(nc.semaphore(name))

        xres = sb("xres", [P, B * TB, D])
        wup_hi, wup_lo = sb("wup_hi", [D, E, 2 * F], F32R), sb("wup_lo", [D, E, 2 * F], F32R)
        wdn_hi, wdn_lo = sb("wdn_hi", [P, CH, D], F32R), sb("wdn_lo", [P, CH, D], F32R)
        wsm_hi, wsm_lo = sb("wsm_hi", [D, CEND], F32R), sb("wsm_lo", [D, CEND], F32R)
        stage = sb("stage", [P, E * 2 * F + CH * D])
        stage_up = stage[:, 0:E * 2 * F].rearrange("p (e f) -> p e f", e=E)
        stage_dn = stage[:, E * 2 * F:].rearrange("p (c d) -> p c d", c=CH)
        probs = stage[:, 0:TB * H * N].rearrange("p (k h n) -> p k h n", k=TB, h=H)
        idn = sb("idn", [P, P])
        near = sb("near", [P, H + 2, P])
        near_t = sb("near_t", [P, H, P])
        dist_sb, dist_t_sb = sb("dist_sb", [P, P]), sb("dist_t_sb", [P, P])
        slope_bc = sb("slope_bc", [P, H])
        rope_sb = sb("rope_sb", [P, 2, N])
        ids = sb("ids", [P, TB, E])
        half_bias = sb("half_bias", [D, 1])
        fbias = sb("fbias", [D, 1])
        pb_row = sb("pb_row", [1, D])
        one_row = sb("one_row", [1, P])
        mhalf = sb("mhalf", [P, TB])
        slope_col = sb("slope_col", [H, 1])
        hid = sb("hid", [P, TB, FT])
        stage_sm = hid[:, 0, 0:CEND]
        gel = sb("gel", [P, 2, F])
        hT_hi, hT_lo = sb("hT_hi", [P, 2, 2 * N], F32R), sb("hT_lo", [P, 2, 2 * N], F32R)
        yT = sb("yT", [D, N])
        bst = [sb(f"bst{w}", [P, TB, 6]) for w in range(3)]
        mv = [sb(f"mv{w}", [P, TB, 2]) for w in range(3)]
        veps = [sb(f"veps{w}", [P, TB]) for w in range(3)]
        rstd = [sb(f"rstd{w}", [P, TB]) for w in range(3)]
        xn = sb("xn", [P, TB, D])
        xT_hi = [sb(f"xT_hi{w}", [D, N], F32R) for w in range(3)]
        xT_lo = [sb(f"xT_lo{w}", [D, N], F32R) for w in range(3)]
        top = [sb(f"top{w}", [P, TB, 8]) for w in range(2)]
        ix = [sb(f"ix{w}", [P, TB, 8], U32) for w in range(2)]
        ixf = [sb(f"ixf{w}", [P, TB, 2]) for w in range(2)]
        nmx = [sb(f"nmx{w}", [P, TB]) for w in range(2)]
        ex = [sb(f"ex{w}", [P, TB, 8]) for w in range(2)]
        sm = [sb(f"sm{w}", [P, TB]) for w in range(2)]
        rs = [sb(f"rs{w}", [P, TB]) for w in range(2)]
        wts = [sb(f"wts{w}", [P, TB, 2]) for w in range(2)]
        eq = [sb(f"eq{w}", [P, 2, TB, E]) for w in range(2)]
        gw = [sb(f"gw{w}", [P, 2, TB, E]) for w in range(2)]
        gate = [sb(f"gate{w}", [P, TB, E]) for w in range(2)]
        rc = sb("rc", [P, 2, N])
        lev = sb("lev", [P, 3, 2, N], BF16)
        qs, ks = sb("qs", [E_ROWS, H, N], BF16), sb("ks", [E_ROWS, H, N], BF16)
        vaug = sb("vaug", [P, TB, H, VW])
        mx = sb("mx", [P, TB, H])
        nm = sb("nm", [P, TB, H])
        ml = sb("ml", [H, 2, N], BF16)
        oT = sb("oT", [P, 2 * N])
        rsn = oT[:, :].rearrange("p (s n) -> p s n", s=2)
        far_v, far_l = rsn[0:H], lev[0:H]
        rden = sb("rden", [P, 2, 4 * TB * 2, 1])
        att = xn
        aT_hi, aT_lo = xT_hi[1], xT_lo[1]

        d_lev = nc.dram_tensor("d_lev", (2, 3, P, N), BF16, kind="Internal").ap()
        d_far = nc.dram_tensor("d_far", (3, 2, H, N), BF16, kind="Internal").ap()
        d_max = nc.dram_tensor("d_max", (2, H, N), BF16, kind="Internal").ap()

        def pb(name):
            return ctx.enter_context(nc.psum_tensor(name, [P, 512], F32))

        psA, psV, psY = pb("psA"), pb("psV"), pb("psY")
        psT = [pb("psT0"), pb("psT1")]
        psS = [pb("psS0"), pb("psS1")]
        psM = pb("psM")

        xin_landed, xrest_landed, small_landed, const_landed = (sem(n) for n in (
            "xin_landed", "xrest_landed", "small_landed", "const_landed"))
        up_landed = [sem(f"up_landed{e}") for e in range(E)]
        down_landed = sem("down_landed")
        wsm_hi_done, wsm_lo_done = sem("wsm_hi_done"), sem("wsm_lo_done")
        wup_hi_done, wup_lo_done = sem("wup_hi_done"), sem("wup_lo_done")
        wdn_hi_done, wdn_lo_done = sem("wdn_hi_done"), sem("wdn_lo_done")
        pool_const, near_done, far_val, far_step = sem("pool_const"), sem("near_done"), sem("far_val"), sem("far_step")
        far_out, rows_landed = sem("far_out"), sem("rows_landed")
        half_done = sem("half_done")
        a_full, v_full, gelu_done, hid_done = sem("a_full"), sem("v_full"), sem("gelu_done"), sem("hid_done")
        hT_full, hT_hi_done, hT_lo_done, down_done = sem("hT_full"), sem("hT_hi_done"), sem("hT_lo_done"), sem("down_done")
        yT_copied, y_full = sem("yT_copied"), sem("y_full")
        y_added, x2_done = sem("y_added"), sem("x2_done")
        LNS = ("f1", "at", "f2")
        stats_done = [sem(f"stats_done_{w}") for w in LNS]
        mean_done = [sem(f"mean_done_{w}") for w in LNS]
        eps_done = [sem(f"eps_done_{w}") for w in LNS]
        rstd_done = [sem(f"rstd_done_{w}") for w in LNS]
        xn_done = [sem(f"xn_done_{w}") for w in LNS]
        xT_full = [sem(f"xT_full_{w}") for w in LNS]
        xT_hi_done = [sem(f"xT_hi_done_{w}") for w in LNS]
        xT_lo_done = [sem(f"xT_lo_done_{w}") for w in LNS]
        logit_full = [sem(f"logit_full{w}") for w in range(2)]
        route = [sem(f"route{w}") for w in range(2)]
        nmx_done = [sem(f"nmx_done{w}") for w in range(2)]
        ex_done = [sem(f"ex_done{w}") for w in range(2)]
        gate_done = [sem(f"gate_done{w}") for w in range(2)]
        v_psum, v_copied = sem("v_psum"), sem("v_copied")
        qk_full, rot_full, cos_done, sin_done = sem("qk_full"), sem("rot_full"), sem("cos_done"), sem("sin_done")
        split_step, lev_out, stack_landed = sem("split_step"), sem("lev_out"), sem("stack_landed")
        s1_full, max_found = sem("s1_full"), sem("max_found")
        nm_done, mT_full, ml_hi, ml_done, ml_out, mrow_landed = (sem(n) for n in (
            "nm_done", "mT_full", "ml_hi", "ml_done", "ml_out", "mrow_landed"))
        s2_full, s2_biased, exp_done = sem("s2_full"), sem("s2_biased"), sem("exp_done")
        pv_full, oT_copied, o_full, rden_done, att_done = (sem(n) for n in (
            "pv_full", "oT_copied", "o_full", "rden_done", "att_done"))
        aT_full, aT_hi_done, aT_lo_done, proj_full = (sem(n) for n in ("aT_full", "aT_hi_done", "aT_lo_done", "proj_full"))
        stored = sem("stored")


        w1_v, v1_v = w1.rearrange("e d f -> d e f"), v1.rearrange("e d f -> d e f")
        w2_v = w2.rearrange("e f d -> (e f) d").rearrange("(c p) d -> p c d", p=P)
        out_v = out.rearrange("b (t p) d -> b p t d", p=P)
        block = ctx.enter_context(nc.Block())

        awaited = {}

        def const_first(eng, const_sem, const, by_batch_sem, value):
            if not isinstance(value, int):
                register = awaited.setdefault(eng, None) or eng.alloc_register("awaited")
                awaited[eng] = register
                eng.reg_mov(register, value)
                value = register
            eng.wait_ge(const_sem, const)
            eng.wait_ge(by_batch_sem, value)

        def iterations(eng, prologue, iteration):
            prologue()
            with eng.Fori(0, B - 2) as g:
                iteration(g, True, True)
            iteration(B - 2, True, False)
            iteration(B - 1, False, False)

        FIRST = (0, 0, True)

        def call_1(g):
            return g * 2 + 1, 1, False

        def call_2(g, more):
            return (g * 2 + 2, 0, False) if more else (g * 2 + 1, 1, False)

        @block.sync
        def _(sp):
            sp.dma_start(xres[:, 0:TB, :], x[0].rearrange("(t p) d -> p t d", p=P)).then_inc(xin_landed, 16)
            sp.dma_start(stage_sm, small_w).then_inc(small_landed, 16)
            sp.dma_start(idn[:, :], ident).then_inc(const_landed, 16)
            sp.dma_start(ids[:, :, :], expert_ids).then_inc(const_landed, 16)
            for e in range(E):
                sp.dma_start(stage_up[:, e, 0:F], w1_v[:, e, :]).then_inc(up_landed[e], 16)
                sp.dma_start(stage_up[:, e, F:2 * F], v1_v[:, e, :]).then_inc(up_landed[e], 16)
            sp.dma_start(stage_dn, w2_v).then_inc(down_landed, 16)
            sp.dma_start(xres[:, TB:, :], x[1:].rearrange("b (t p) d -> p (b t) d", p=P)).then_inc(xrest_landed, 16)
            sp.wait_ge(far_step, 5)
            sp.dma_start(d_far.rearrange("l s h n -> h l s n"), far_l).then_inc(far_out, 16)
            sp.wait_ge(far_out, 16)
            sp.dma_start(ks[QK_ROWS:QK_ROWS + 3, :, :], d_far[:, 0]).then_inc(rows_landed, 16)
            sp.dma_start(qs[QK_ROWS + 3:S_ROWS, :, :], d_far[:, 1]).then_inc(rows_landed, 16)

            def stack(b):
                sp.wait_ge(split_step, b * 5 + 5)
                for s in range(2):
                    sp.dma_start(d_lev[s].rearrange("l p n -> p l n"), lev[:, :, s, :]).then_inc(lev_out, 16)
                sp.wait_ge(lev_out, b * 32 + 32)
                for s, dst in ((0, qs), (1, ks)):
                    for t, pair in enumerate(PAIRS):
                        sp.dma_start(dst[t * HD:(t + 1) * HD, :, :],
                                     d_lev[s, pair[s]].rearrange("(d h) n -> d h n", h=H)).then_inc(stack_landed, 16)

            def prologue():
                stack(0)

            def iteration(g, more, more2):
                sp.wait_ge(ml_done, g + 1)
                sp.dma_start(d_max.rearrange("l h n -> h l n"), ml[:, :, :]).then_inc(ml_out, 16)
                sp.wait_ge(ml_out, g * 16 + 16)
                sp.dma_start(qs[S_ROWS:E_ROWS, :, :], d_max).then_inc(mrow_landed, 16)
                if more:
                    stack(g + 1)
                sp.wait_ge(y_added, call_2(g, more)[0] + 1)
                sp.dma_start(out_v[g], xres[:, bass.ds(g * TB, TB), :]).then_inc(stored, 16)

            iterations(sp, prologue, iteration)
            sp.wait_ge(stored, B * 16)

        @block.gpsimd
        def _(pool):
            nc.gpsimd.memset(mhalf[:, :], -0.5)
            nc.gpsimd.memset(one_row[:, :], 1.0)
            nc.gpsimd.memset(near[:, :, :], 0.0)
            nc.gpsimd.memset(vaug[:, :, :, :], 0.0).then_inc(far_val, 1)
            pool.wait_ge(far_val, 1)
            nc.gpsimd.memset(vaug[:, :, :, HD:HD + 1], 1.0).then_inc(half_done, 1)
            pool.wait_ge(pool_const, 96)

            def rstd_of(w, b):
                const_first(pool, half_done, 1, mean_done[w], b * TB + TB)
                nc.gpsimd.tensor_scalar(veps[w][:, :], mv[w][:, :, 1], EPS, None, ALU.add).then_inc(eps_done[w], 1)
                pool.wait_ge(eps_done[w], b + 1)
                nc.gpsimd.tensor_tensor(rstd[w][:, :], veps[w][:, :], mhalf[:, :], ALU.pow).then_inc(rstd_done[w], 1)

            def split_qk(b):
                pool.wait_ge(cos_done, b + 1)
                pool.wait_ge(sin_done, b + 1)
                nc.gpsimd.tensor_tensor(rc[:, :, :], rc[:, :, :], rsn, ALU.add).then_inc(split_step, 1)
                const_first(pool, far_out, 16, split_step, b * 5 + 1)
                nc.gpsimd.tensor_copy(lev[:, 0], rc[:, :, :]).then_inc(split_step, 1)
                pool.wait_ge(split_step, b * 5 + 2)
                nc.gpsimd.tensor_tensor(rc[:, :, :], rc[:, :, :], lev[:, 0], ALU.subtract).then_inc(split_step, 1)
                const_first(pool, far_out, 16, split_step, b * 5 + 3)
                nc.gpsimd.tensor_copy(lev[:, 1], rc[:, :, :]).then_inc(split_step, 1)
                pool.wait_ge(split_step, b * 5 + 4)
                nc.gpsimd.tensor_tensor(lev[:, 2], rc[:, :, :], lev[:, 1], ALU.subtract).then_inc(split_step, 1)

            def prologue():
                rstd_of(0, 0)
                nc.gpsimd.tensor_scalar(half_bias[:, :], fbias[:, :], 0.5, None, ALU.mult).then_inc(half_done, 1)
                rstd_of(0, 1)
                for h in range(H):
                    nc.gpsimd.tensor_scalar(near[:, h + 1, :], dist_sb[:, :], slope_bc[:, h:h + 1], 8.0,
                                            ALU.mult, ALU.mult).then_inc(near_done, 1)
                    nc.gpsimd.tensor_scalar(near_t[:, h, :], dist_t_sb[:, :], slope_bc[:, h:h + 1], 8.0,
                                            ALU.mult, ALU.mult).then_inc(near_done, 1)
                nc.gpsimd.tensor_scalar(far_v, far_v, slope_col[:, :], 8.0, ALU.mult, ALU.mult).then_inc(far_step, 1)
                pool.wait_ge(far_step, 1)
                nc.gpsimd.tensor_copy(far_l[:, 0], far_v).then_inc(far_step, 1)
                pool.wait_ge(far_step, 2)
                nc.gpsimd.tensor_tensor(far_v, far_v, far_l[:, 0], ALU.subtract).then_inc(far_step, 1)
                pool.wait_ge(far_step, 3)
                nc.gpsimd.tensor_copy(far_l[:, 1], far_v).then_inc(far_step, 1)
                pool.wait_ge(far_step, 4)
                nc.gpsimd.tensor_tensor(far_l[:, 2], far_v, far_l[:, 1], ALU.subtract).then_inc(far_step, 1)
                pool.wait_ge(far_out, 16)
                rstd_of(1, 0)
                split_qk(0)

            def iteration(g, more, more2):
                if more2:
                    rstd_of(0, g + 2)
                rstd_of(2, g)
                if more:
                    rstd_of(1, g + 1)
                    split_qk(g + 1)

            iterations(pool, prologue, iteration)

        @block.scalar
        def _(act):
            act.dma_start(slope_bc[:, :], slopes.partition_broadcast(P)).then_inc(pool_const, 16)
            act.dma_start(dist_sb[:, :], dist).then_inc(pool_const, 16)
            act.dma_start(dist_t_sb[:, :], dist_t).then_inc(pool_const, 16)
            act.dma_start(fbias[:, :], ffn_bias.rearrange("(d o) -> d o", o=1)).then_inc(pool_const, 16)
            act.dma_start(slope_col[:, :], slopes.rearrange("(h o) -> h o", o=1)).then_inc(pool_const, 16)
            act.dma_start(far_v, far).then_inc(pool_const, 16)
            act.dma_start(rope_sb[:, :, :], rope).then_inc(const_landed, 16)
            act.dma_start(pb_row[:, :], proj_b.rearrange("(o d) -> o d", o=1)).then_inc(const_landed, 16)
            act.dma_start(qs[QK_ROWS:QK_ROWS + 3, :, :], ones_rows[0:3]).then_inc(rows_landed, 16)
            act.dma_start(ks[QK_ROWS + 3:E_ROWS, :, :], ones_rows[3:8]).then_inc(rows_landed, 16)
            copy, gelu, exp, ident_f = ACT.Copy, ACT.Gelu, ACT.Exp, ACT.Identity

            def xT_high(w, b):
                act.wait_ge(xT_full[w], b + 1)
                nc.scalar.activation(xT_hi[w][:, :], psM[:, 0:N], copy).then_inc(xT_hi_done[w], 1)

            def router_exp(r, b):
                act.wait_ge(nmx_done[r], b + 1)
                for t in range(TB):
                    nc.scalar.activation(ex[r][:, t, :], top[r][:, t, :], exp, bias=nmx[r][:, t:t + 1],
                                         accum_out=sm[r][:, t:t + 1]).then_inc(ex_done[r], 1)

            def gate_gelu(c, u):
                act.wait_ge(a_full, c[0] * UNITS + (u + 1))
                if u >= 2 or not c[2]:
                    act.wait_ge(hid_done, c[0] * UNITS + (u - 1))
                nc.scalar.activation(gel[:, u % 2, :], psA[:, 0:F], gelu).then_inc(gelu_done, 1)

            def hid_high(c, k):
                act.wait_ge(hT_full, c[0] * STEPS + (k + 1))
                s = (k + c[1]) % 2
                if k >= 2 or not c[2]:
                    act.wait_ge(down_done, c[0] * STEPS + (k - 1))
                nc.scalar.activation(hT_hi[:, s, :], psT[s][:, :], copy).then_inc(hT_hi_done, 1)

            def y_copy(c):
                act.wait_ge(down_done, c[0] * STEPS + STEPS)
                nc.scalar.activation(yT[:, :], psY[:, 0:N], ident_f, bias=half_bias[:, 0:1]).then_inc(yT_copied, 1)

            def values(b):
                act.wait_ge(v_psum, b + 1)
                nc.scalar.activation(vaug[:, :, :, 0:HD],
                                     psM[:, N:2 * N].rearrange("p (t h d) -> p t h d", t=TB, h=H), copy).then_inc(v_copied, 1)

            def max_high(b):
                act.wait_ge(mT_full, b + 1)
                nc.scalar.activation(ml[:, 0, :], psM[0:H, 0:N], copy).then_inc(ml_hi, 1)

            def attention_exp(b, j):
                act.wait_ge(s2_biased, b * 16 + (j + 1))
                hp, kt = j // 2, j % 2
                nc.scalar.activation(probs[:, kt, 2 * hp:2 * hp + 2, :],
                                     psS[j % 2][:, :].rearrange("p (h n) -> p h n", h=2), exp).then_inc(exp_done, 1)

            def oT_copy(b, half):
                act.wait_ge(pv_full, b * 2 + (half + 1))
                nc.scalar.activation(oT[:, :], psM[:, :], copy).then_inc(oT_copied, 1)

            def aT_high(b):
                act.wait_ge(aT_full, b + 1)
                nc.scalar.activation(aT_hi[:, :], psM[:, 0:N], copy).then_inc(aT_hi_done, 1)

            def prologue():
                act.wait_ge(small_landed, 16)
                nc.scalar.activation(wsm_hi[:, :], stage_sm, copy).then_inc(wsm_hi_done, 1)
                xT_high(0, 0)
                router_exp(0, 0)
                for e in range(E):
                    act.wait_ge(up_landed[e], 32)
                    nc.scalar.activation(wup_hi[:, e, :], stage_up[:, e, :], copy).then_inc(wup_hi_done, 1)
                    for u in (2 * e, 2 * e + 1):
                        gate_gelu(FIRST, u)
                act.wait_ge(down_landed, 16)
                nc.scalar.activation(wdn_hi[:, :, :], stage_dn, copy).then_inc(wdn_hi_done, 1)
                act.wait_ge(half_done, 2)
                for k in range(STEPS):
                    hid_high(FIRST, k)
                    if k == 3:
                        xT_high(0, 1)
                    if k == 5:
                        router_exp(0, 1)
                y_copy(FIRST)
                xT_high(1, 0)
                values(0)

            def iteration(g, more, more2):
                c1, c2 = call_1(g), call_2(g, more)
                for u in range(UNITS):
                    if more:
                        gate_gelu(c1, u)
                    if u == M_AT:
                        max_high(g)
                for j in range(16):
                    attention_exp(g, j)
                    if more and j % 2 == 0:
                        hid_high(c1, j // 2)
                    if more2 and j == LN_AT:
                        xT_high(0, g + 2)
                    if more2 and j == LN_AT + 3:
                        router_exp(0, g + 2)
                    if j == PV_AT:
                        oT_copy(g, 0)
                oT_copy(g, 1)
                if more:
                    hid_high(c1, 8)
                aT_high(g)
                if more:
                    hid_high(c1, 9)
                    hid_high(c1, 10)
                xT_high(2, g)
                if more:
                    y_copy(c1)
                router_exp(1, g)
                for u in range(UNITS):
                    gate_gelu(c2, u)
                    if more and u == XT_AT:
                        xT_high(1, g + 1)
                    if more and u == V_AT:
                        values(g + 1)
                for k in range(STEPS):
                    hid_high(c2, k)
                y_copy(c2)

            iterations(act, prologue, iteration)

        @block.vector
        def _(dve):
            def ln_stats(w, b):
                for t in range(TB):
                    nc.vector.bn_stats(bst[w][:, t, :], xres[:, b * TB + t, :]).then_inc(stats_done[w], 1)
                for t in range(TB):
                    const_first(dve, xin_landed, 16, stats_done[w], b * TB + (t + 1))
                    nc.vector.bn_aggr(mv[w][:, t, :], bst[w][:, t, :]).then_inc(mean_done[w], 1)

            def ln_apply(w, b):
                dve.wait_ge(rstd_done[w], b + 1)
                for t in range(TB):
                    nc.vector.tensor_scalar(xn[:, t, :], xres[:, b * TB + t, :], mv[w][:, t, 0:1], rstd[w][:, t:t + 1],
                                            ALU.subtract, ALU.mult).then_inc(xn_done[w], 1)

            def xT_low(w, b):
                dve.wait_ge(xT_hi_done[w], b + 1)
                nc.vector.tensor_tensor(xT_lo[w][:, :], psM[:, 0:N], xT_hi[w][:, :].bitcast(F32), ALU.subtract).then_inc(
                    xT_lo_done[w], 1)

            def route_top(r, b):
                const_first(dve, const_landed, 64, logit_full[r], b + 1)
                for t in range(TB):
                    nc.vector.max(top[r][:, t, :], psM[:, N + 8 * t:N + 8 * t + 8]).then_inc(route[r], 1)
                dve.wait_ge(route[r], b * ROUTE + 2)
                nc.vector.tensor_scalar(nmx[r][:, :], top[r][:, :, 0], -1.0, None, ALU.mult).then_inc(nmx_done[r], 1)
                for t in range(TB):
                    nc.vector.max_index(ix[r][:, t, :], top[r][:, t, :], psM[:, N + 8 * t:N + 8 * t + 8]).then_inc(route[r], 1)
                dve.wait_ge(route[r], b * ROUTE + 4)
                nc.vector.tensor_copy(ixf[r][:, :, :], ix[r][:, :, 0:2]).then_inc(route[r], 1)

            def route_gate(r, b):
                dve.wait_ge(route[r], b * ROUTE + 5)
                nc.vector.tensor_tensor(eq[r][:, :, :, :], ids[:, None, :, :].broadcast_to([P, 2, TB, E]),
                                        ixf[r][:, :, :].rearrange("p t k -> p k t")[:, :, :, None].broadcast_to([P, 2, TB, E]),
                                        ALU.is_equal).then_inc(route[r], 1)
                dve.wait_ge(ex_done[r], b * TB + TB)
                nc.vector.tensor_scalar(sm[r][:, :], sm[r][:, :], 2.0, None, ALU.mult).then_inc(route[r], 1)
                dve.wait_ge(route[r], b * ROUTE + 7)
                nc.vector.reciprocal(rs[r][:, :], sm[r][:, :]).then_inc(route[r], 1)
                dve.wait_ge(route[r], b * ROUTE + 8)
                nc.vector.tensor_tensor(wts[r][:, :, :], ex[r][:, :, 0:2], rs[r][:, :, None].broadcast_to([P, TB, 2]),
                                        ALU.mult).then_inc(route[r], 1)
                dve.wait_ge(route[r], b * ROUTE + 9)
                nc.vector.tensor_tensor(gw[r][:, :, :, :], eq[r][:, :, :, :],
                                        wts[r][:, :, :].rearrange("p t k -> p k t")[:, :, :, None].broadcast_to([P, 2, TB, E]),
                                        ALU.mult).then_inc(route[r], 1)
                dve.wait_ge(route[r], b * ROUTE + 10)
                nc.vector.tensor_tensor(gate[r][:, :, :], gw[r][:, 0], gw[r][:, 1], ALU.add).then_inc(gate_done[r], 1)

            def gated(r, b, c, u):
                e, t = u // TB, u % TB
                if u == 0:
                    dve.wait_ge(gate_done[r], b + 1)
                    if not c[2]:
                        dve.wait_ge(hT_full, c[0] * STEPS)
                dve.wait_ge(gelu_done, c[0] * UNITS + (u + 1))
                dve.wait_ge(v_full, c[0] * UNITS + (u + 1))
                nc.vector.scalar_tensor_tensor(out=hid[:, t, e * F:(e + 1) * F], in0=psV[:, 0:F],
                                               scalar=gate[r][:, t, e:e + 1], in1=gel[:, u % 2, :],
                                               op0=ALU.mult, op1=ALU.mult).then_inc(hid_done, 1)

            def hid_low(c, k):
                dve.wait_ge(hT_hi_done, c[0] * STEPS + (k + 1))
                s = (k + c[1]) % 2
                nc.vector.tensor_tensor(hT_lo[:, s, :], psT[s][:, :], hT_hi[:, s, :].bitcast(F32), ALU.subtract).then_inc(
                    hT_lo_done, 1)

            def y_add(c, b):
                dve.wait_ge(y_full, c[0] + 1)
                nc.vector.tensor_tensor(xres[:, bass.ds(b * TB, TB), :], xres[:, bass.ds(b * TB, TB), :],
                                        psY[:, N:2 * N].rearrange("p (t d) -> p t d", t=TB), ALU.add).then_inc(y_added, 1)

            def rotate(b):
                dve.wait_ge(qk_full, b + 1)
                if not (isinstance(b, int) and b == 0):
                    dve.wait_ge(split_step, b * 5)
                nc.vector.tensor_tensor(rc[:, :, :], psM[:, :].rearrange("p (s n) -> p s n", s=2), rope_sb[:, 0:1, :].broadcast_to([P, 2, N]), ALU.mult
                                        ).then_inc(cos_done, 1)

            def rotate_2(b):
                dve.wait_ge(rot_full, b + 1)
                nc.vector.tensor_tensor(rsn, psM[:, :].rearrange("p (s n) -> p s n", s=2), rope_sb[:, 1:2, :].broadcast_to([P, 2, N]), ALU.mult
                                        ).then_inc(sin_done, 1)

            def row_max(b, i):
                qt, hp = i // 8, i % 8
                const_first(dve, near_done, 2 * H, s1_full, b * 16 + (i + 1))
                for j in range(2):
                    h = 2 * hp + j
                    bias = near[:, h + 1:H + 2:H - h, :] if qt == 0 else near[:, 0:h + 2:h + 1, :]
                    part = psS[i % 2][:, j * N:(j + 1) * N].rearrange("p (a n) -> p a n", a=TB)
                    nc.vector.tensor_tensor_reduce(out=part, in0=part, in1=bias,
                                                   scale=1.0, scalar=-3.0e38, op0=ALU.add, op1=ALU.max,
                                                   accum_out=mx[:, qt, h:h + 1]).then_inc(max_found, 1)

            def max_negate(b):
                dve.wait_ge(max_found, b * 32 + 32)
                nc.vector.tensor_scalar(nm[:, :, :], mx[:, :, :], -1.0, None, ALU.mult).then_inc(nm_done, 1)

            def max_low(b):
                dve.wait_ge(ml_hi, b + 1)
                nc.vector.tensor_tensor(ml[:, 1, :], psM[0:H, 0:N], ml[:, 0, :], ALU.subtract).then_inc(ml_done, 1)

            def near_bias(b, j):
                hp, kt = j // 2, j % 2
                dve.wait_ge(s2_full, b * 16 + (j + 1))
                part = psS[j % 2][:, :].rearrange("p (h n) -> p h n", h=2)[:, :, kt * P:(kt + 1) * P]
                nc.vector.tensor_tensor(part, part, near_t[:, 2 * hp:2 * hp + 2, :], ALU.add).then_inc(s2_biased, 1)

            def normalize(b, half):
                dve.wait_ge(o_full, b * 2 + (half + 1))
                nc.vector.reciprocal(rden[:, half], psM[:, :].rearrange("p (x v) -> p x v", v=VW)[:, :, HD:HD + 1]
                                     ).then_inc(rden_done, 1)
                dve.wait_ge(rden_done, b * 2 + (half + 1))
                for qt in range(TB):
                    o = psM[:, :].rearrange("p (a q j v) -> p a q j v", a=2, q=TB, j=4)[:, :, qt, :, 0:HD]
                    r = rden[:, half].rearrange("p (a q j) o -> p a q j o", a=2, q=TB)[:, :, qt, :, :].broadcast_to([P, 2, 4, HD])
                    nc.vector.tensor_tensor(att[:, qt, half * 64:(half + 1) * 64].rearrange("p (a j d) -> p a j d", a=2, j=4),
                                            o, r, ALU.mult).then_inc(att_done, 1)

            def aT_low(b):
                dve.wait_ge(aT_hi_done, b + 1)
                nc.vector.tensor_tensor(aT_lo[:, :], psM[:, 0:N], aT_hi[:, :].bitcast(F32), ALU.subtract).then_inc(aT_lo_done, 1)

            def attention_add(b):
                dve.wait_ge(proj_full, b + 1)
                nc.vector.tensor_tensor(xres[:, bass.ds(b * TB, TB), :], xres[:, bass.ds(b * TB, TB), :],
                                        psM[:, 0:N].rearrange("p (t d) -> p t d", t=TB), ALU.add).then_inc(x2_done, 1)

            def prologue():
                dve.wait_ge(xin_landed, 16)
                ln_stats(0, 0)
                ln_apply(0, 0)
                dve.wait_ge(wsm_hi_done, 1)
                nc.vector.tensor_tensor(wsm_lo[:, :], stage_sm, wsm_hi[:, :].bitcast(F32), ALU.subtract).then_inc(wsm_lo_done, 1)
                xT_low(0, 0)
                route_top(0, 0)
                route_gate(0, 0)
                for e in range(E):
                    dve.wait_ge(wup_hi_done, e + 1)
                    nc.vector.tensor_tensor(wup_lo[:, e, :], stage_up[:, e, :], wup_hi[:, e, :].bitcast(F32), ALU.subtract
                                            ).then_inc(wup_lo_done, 1)
                    for u in (2 * e, 2 * e + 1):
                        gated(0, 0, FIRST, u)
                dve.wait_ge(xrest_landed, 16)
                ln_stats(0, 1)
                dve.wait_ge(wdn_hi_done, 1)
                nc.vector.tensor_tensor(wdn_lo[:, :, :], stage_dn, wdn_hi[:, :, :].bitcast(F32), ALU.subtract).then_inc(wdn_lo_done, 1)
                ln_apply(0, 1)
                for k in range(STEPS):
                    hid_low(FIRST, k)
                    if k == 3:
                        xT_low(0, 1)
                    if k == 4:
                        route_top(0, 1)
                    if k == 6:
                        route_gate(0, 1)
                y_add(FIRST, 0)
                dve.wait_ge(y_added, 1)
                ln_stats(1, 0)
                ln_apply(1, 0)
                xT_low(1, 0)
                rotate(0)
                dve.wait_ge(far_step, 5)
                rotate_2(0)
                for i in range(P1A):
                    row_max(0, i)

            def iteration(g, more, more2):
                c1, c2 = call_1(g), call_2(g, more)
                for u in range(UNITS):
                    if more:
                        gated(0, g + 1, c1, u)
                    if u < 16 - P1A:
                        row_max(g, P1A + u)
                    if u == 16 - P1A:
                        max_negate(g)
                    if u == M_AT:
                        max_low(g)
                if more2:
                    ln_stats(0, g + 2)
                    ln_apply(0, g + 2)
                for j in range(16):
                    near_bias(g, j)
                    if more and j % 2 == 0:
                        hid_low(c1, j // 2)
                    if more2 and j == LN_AT:
                        xT_low(0, g + 2)
                    if more2 and j == LN_AT + 2:
                        route_top(0, g + 2)
                    if more2 and j == LN_AT + 5:
                        route_gate(0, g + 2)
                    if j == O_AT:
                        normalize(g, 0)
                if more:
                    hid_low(c1, 8)
                normalize(g, 1)
                aT_low(g)
                if more:
                    hid_low(c1, 9)
                attention_add(g)
                const_first(dve, xin_landed, 16, x2_done, g + 1)
                ln_stats(2, g)
                if more:
                    hid_low(c1, 10)
                ln_apply(2, g)
                xT_low(2, g)
                route_top(1, g)
                if more:
                    y_add(c1, g + 1)
                route_gate(1, g)
                for u in range(UNITS):
                    gated(1, g, c2, u)
                    if more and u == 0:
                        const_first(dve, xin_landed, 16, y_added, c1[0] + 1)
                        ln_stats(1, g + 1)
                    if more and u == 2:
                        ln_apply(1, g + 1)
                    if more and u == XT_AT:
                        xT_low(1, g + 1)
                    if more and u == QK_AT:
                        rotate(g + 1)
                    if more and u == QK_AT + 2:
                        rotate_2(g + 1)
                for k in range(STEPS):
                    hid_low(c2, k)
                    if more and k >= STEPS - P1A:
                        row_max(g + 1, k - (STEPS - P1A))
                y_add(c2, g)

            iterations(dve, prologue, iteration)

        @block.tensor
        def _(pe):
            def mm3(o, l_hi, l_lo, r_hi, r_lo, start=True, stop=True):
                nc.tensor.matmul(o, l_hi, r_hi, start=start, stop=False)
                nc.tensor.matmul(o, l_hi, r_lo, start=False, stop=False)
                return nc.tensor.matmul(o, l_lo, r_hi, start=False, stop=stop)

            def ln_T(w, b):
                pe.wait_ge(xn_done[w], b * TB + TB)
                for t in range(TB):
                    i = nc.tensor.transpose(psM[:, t * P:(t + 1) * P], xn[:, t, :], idn[:, :])
                i.then_inc(xT_full[w], 1)

            def logits(r, b):
                w = 2 * r
                pe.wait_ge(xT_lo_done[w], b + 1)
                for t in range(TB):
                    s = slice(t * P, (t + 1) * P)
                    i = mm3(psM[:, N + 8 * t:N + 8 * t + 8], xT_hi[w][:, s], xT_lo[w][:, s], wsm_hi[:, CR:CEND], wsm_lo[:, CR:CEND])
                i.then_inc(logit_full[r], 1)

            def up_gate(r, c, u):
                e, t, w = u // TB, u % TB, 2 * r
                if not (c[2] and u == 0):
                    pe.wait_ge(gelu_done, c[0] * UNITS + u)
                s = slice(t * P, (t + 1) * P)
                mm3(psA[:, 0:F], xT_hi[w][:, s], xT_lo[w][:, s], wup_hi[:, e, 0:F], wup_lo[:, e, 0:F]).then_inc(a_full, 1)

            def up_value(r, c, u):
                e, t, w = u // TB, u % TB, 2 * r
                if not (c[2] and u == 0):
                    pe.wait_ge(hid_done, c[0] * UNITS + u)
                s = slice(t * P, (t + 1) * P)
                mm3(psV[:, 0:F], xT_hi[w][:, s], xT_lo[w][:, s], wup_hi[:, e, F:2 * F], wup_lo[:, e, F:2 * F]).then_inc(v_full, 1)

            def down_T(c, k):
                units = min(UNITS, ((2 * k + 2) * P + F - 1) // F * TB)
                pe.wait_ge(hid_done, c[0] * UNITS + units)
                s = (k + c[1]) % 2
                if k >= 2 or not c[2]:
                    pe.wait_ge(hT_lo_done, c[0] * STEPS + (k - 1))
                for a in range(2):
                    for t in range(TB):
                        ch = 2 * k + a
                        i = nc.tensor.transpose(psT[s][:, (a * TB + t) * P:(a * TB + t + 1) * P],
                                                hid[:, t, ch * P:(ch + 1) * P], idn[:, :])
                i.then_inc(hT_full, 1)

            def down_mm(c, k):
                pe.wait_ge(hT_lo_done, c[0] * STEPS + (k + 1))
                if k == 0 and not c[2]:
                    pe.wait_ge(y_added, c[0])
                s = (k + c[1]) % 2
                for a in range(2):
                    ch = 2 * k + a
                    r_hi, r_lo = hT_hi[:, s, a * N:(a + 1) * N], hT_lo[:, s, a * N:(a + 1) * N]
                    nc.tensor.matmul(psY[:, 0:N], wdn_hi[:, ch, :], r_hi, start=(ch == 0), stop=False)
                    nc.tensor.matmul(psY[:, 0:N], wdn_hi[:, ch, :], r_lo, start=False, stop=False)
                    i = nc.tensor.matmul(psY[:, 0:N], wdn_lo[:, ch, :], r_hi, start=False, stop=(ch == CH - 1))
                i.then_inc(down_done, 1)

            def y_T(c):
                pe.wait_ge(yT_copied, c[0] + 1)
                for t in range(TB):
                    i = nc.tensor.transpose(psY[:, N + t * P:N + (t + 1) * P], yT[:, t * P:(t + 1) * P], idn[:, :])
                i.then_inc(y_full, 1)

            def value_mm(b):
                pe.wait_ge(xT_lo_done[1], b + 1)
                for t in range(TB):
                    s = slice(t * P, (t + 1) * P)
                    i = mm3(psM[:, N + t * P:N + (t + 1) * P], xT_hi[1][:, s], xT_lo[1][:, s],
                            wsm_hi[:, CV:CV + P], wsm_lo[:, CV:CV + P])
                i.then_inc(v_psum, 1)

            def qk_mm(first, full):
                for s in range(2):
                    c = slice(first + s * P, first + (s + 1) * P)
                    i = mm3(psM[:, s * N:(s + 1) * N], wsm_hi[:, c], wsm_lo[:, c], xT_hi[1][:, :], xT_lo[1][:, :])
                i.then_inc(full, 1)

            def qk(b):
                pe.wait_ge(v_copied, b + 1)
                qk_mm(CQ, qk_full)

            def rot(b):
                pe.wait_ge(cos_done, b + 1)
                qk_mm(CQR, rot_full)

            def scores_1(b, i):
                qt, hp = i // 8, i % 8
                if i == 0:
                    pe.wait_ge(stack_landed, b * (16 * 2 * len(PAIRS)) + 16 * 2 * len(PAIRS))
                    if not (isinstance(b, int) and b == 0):
                        pe.wait_ge(exp_done, b * 16)
                if i >= 2:
                    pe.wait_ge(max_found, b * 32 + 2 * (i - 1))
                for j in range(2):
                    h = 2 * hp + j
                    m = nc.tensor.matmul(psS[i % 2][:, j * N:(j + 1) * N], qs[0:S_ROWS, h, qt * P:(qt + 1) * P],
                                         ks[0:S_ROWS, h, :], start=True, stop=True)
                m.then_inc(s1_full, 1)

            def max_T(b):
                pe.wait_ge(nm_done, b + 1)
                pe.wait_ge(sin_done, b + 1)
                for t in range(TB):
                    i = nc.tensor.transpose(psM[0:H, t * P:(t + 1) * P], nm[:, t, :], idn[:, :])
                i.then_inc(mT_full, 1)

            def scores_2(b, j):
                hp, kt = j // 2, j % 2
                if j == 0:
                    pe.wait_ge(mrow_landed, b * 16 + 16)
                    pe.wait_ge(max_found, b * 32 + 32)
                if j >= 2:
                    pe.wait_ge(exp_done, b * 16 + (j - 1))
                for a in range(2):
                    h = 2 * hp + a
                    m = nc.tensor.matmul(psS[j % 2][:, a * N:(a + 1) * N], ks[0:E_ROWS, h, kt * P:(kt + 1) * P],
                                         qs[0:E_ROWS, h, :], start=True, stop=True)
                m.then_inc(s2_full, 1)

            def weighted_values(b, half):
                pe.wait_ge(exp_done, b * 16 + 8 * (half + 1))
                if half == 0:
                    pe.wait_ge(ml_done, b + 1)
                else:
                    pe.wait_ge(att_done, b * 4 + 2)
                for a in range(2):
                    for kt in range(TB):
                        for j in range(4):
                            h = half * 8 + a * 4 + j
                            m = nc.tensor.matmul(psM[j * VW:(j + 1) * VW, a * N:(a + 1) * N], vaug[:, kt, h, :],
                                                 probs[:, kt, h, :], start=(kt == 0), stop=(kt == TB - 1),
                                                 tile_position=(0, j * VW))
                m.then_inc(pv_full, 1)

            def out_T(b, half):
                pe.wait_ge(oT_copied, b * 2 + (half + 1))
                for x4 in range(4):
                    m = nc.tensor.transpose(psM[:, x4 * P:(x4 + 1) * P], oT[:, x4 * P:(x4 + 1) * P], idn[:, :])
                m.then_inc(o_full, 1)

            def att_T(b):
                pe.wait_ge(att_done, b * 4 + 4)
                for t in range(TB):
                    m = nc.tensor.transpose(psM[:, t * P:(t + 1) * P], att[:, t, :], idn[:, :])
                m.then_inc(aT_full, 1)

            def project(b):
                pe.wait_ge(aT_lo_done, b + 1)
                for t in range(TB):
                    s, o = slice(t * P, (t + 1) * P), psM[:, t * P:(t + 1) * P]
                    mm3(o, aT_hi[:, s], aT_lo[:, s], wsm_hi[:, CP:CP + P], wsm_lo[:, CP:CP + P], stop=False)
                    m = nc.tensor.matmul(o, one_row[:, :], pb_row[:, :], start=False, stop=True)
                m.then_inc(proj_full, 1)

            def prologue():
                pe.wait_ge(const_landed, 64)
                ln_T(0, 0)
                pe.wait_ge(wsm_lo_done, 1)
                logits(0, 0)
                for u in range(UNITS):
                    if u % TB == 0:
                        pe.wait_ge(wup_lo_done, u // TB + 1)
                    up_gate(0, FIRST, u)
                    up_value(0, FIRST, u)
                pe.wait_ge(wdn_lo_done, 1)
                for k in range(STEPS):
                    down_T(FIRST, k)
                    if k >= 1:
                        down_mm(FIRST, k - 1)
                    if k == 2:
                        pe.wait_ge(gate_done[0], 1)
                        ln_T(0, 1)
                    if k == 4:
                        logits(0, 1)
                down_mm(FIRST, STEPS - 1)
                y_T(FIRST)
                pe.wait_ge(gate_done[0], 2)
                ln_T(1, 0)
                value_mm(0)
                qk(0)
                rot(0)
                pe.wait_ge(rows_landed, 64)
                for i in range(P1A):
                    scores_1(0, i)

            def iteration(g, more, more2):
                c1, c2 = call_1(g), call_2(g, more)
                for u in range(UNITS):
                    if more:
                        up_gate(0, c1, u)
                    if u < 16 - P1A:
                        scores_1(g, P1A + u)
                    if u == M_AT:
                        max_T(g)
                    if more:
                        up_value(0, c1, u)
                for j in range(16):
                    if more and j % 2 == 0:
                        down_T(c1, j // 2)
                    scores_2(g, j)
                    if more and j % 2 == 1 and j >= 3:
                        down_mm(c1, j // 2 - 1)
                    if more2 and j == LN_AT:
                        pe.wait_ge(ml_done, g + 1)
                        ln_T(0, g + 2)
                    if more2 and j == LN_AT + 1:
                        logits(0, g + 2)
                    if j == PV_AT:
                        if more2:
                            pe.wait_ge(route[0], (g + 2) * ROUTE + 4)
                        weighted_values(g, 0)
                    if j == O_AT:
                        out_T(g, 0)
                if more:
                    down_T(c1, 8)
                    down_mm(c1, 7)
                weighted_values(g, 1)
                if more:
                    down_T(c1, 9)
                out_T(g, 1)
                if more:
                    down_mm(c1, 8)
                att_T(g)
                if more:
                    down_T(c1, 10)
                    down_mm(c1, 9)
                project(g)
                if more:
                    down_mm(c1, 10)
                pe.wait_ge(x2_done, g + 1)
                ln_T(2, g)
                if more:
                    y_T(c1)
                logits(1, g)
                for u in range(UNITS):
                    up_gate(1, c2, u)
                    if more and u == XT_AT:
                        pe.wait_ge(route[1], g * ROUTE + 4)
                        ln_T(1, g + 1)
                    if more and u == V_AT:
                        value_mm(g + 1)
                    if more and u == QK_AT:
                        qk(g + 1)
                    if more and u == QK_AT + 1:
                        rot(g + 1)
                    up_value(1, c2, u)
                for k in range(STEPS):
                    down_T(c2, k)
                    if more and k >= STEPS - P1A:
                        scores_1(g + 1, k - (STEPS - P1A))
                    if k >= 1:
                        down_mm(c2, k - 1)
                down_mm(c2, STEPS - 1)
                y_T(c2)

            iterations(pe, prologue, iteration)


def _constants():
    import numpy as np

    ident = np.eye(P, dtype=np.float32)
    pos = np.arange(N)
    dist = np.minimum(pos[None, :P] - pos[:P, None], 0).astype(np.float32)
    inv = (np.float32(1.0) / np.float32(10000.0) ** (np.arange(0, HD, 2, dtype=np.float32) / np.float32(HD))).astype(np.float32)
    angle = (pos.astype(np.float32)[None, :] * inv[:, None]).astype(np.float64)
    d = np.arange(HD)
    cos = np.cos(angle)[d % (HD // 2)]
    sin = np.sin(angle)[d % (HD // 2)] * np.where(d < HD // 2, -1.0, 1.0)[:, None]
    rope = np.stack([cos, sin], 1)[:, None] * HD ** -0.25
    rope = np.broadcast_to(rope, (HD, H, 2, N)).reshape(P, 2, N).astype(np.float32)
    ids = np.broadcast_to(np.arange(E, dtype=np.float32), (P, TB, E))
    key, query = np.where(pos < P, pos - (P - 1), 0), np.where(pos >= P, (P - 1) - pos, 0)
    far = np.broadcast_to(np.stack([key, query]).astype(np.float32), (H, 2, N))
    rows = np.stack([pos >= P] * 3 + [pos < P] * 3 + [pos >= 0] * 2).astype(np.dtype("bfloat16"))
    rows = np.broadcast_to(rows[:, None, :], (8, H, N))
    return [np.ascontiguousarray(a) for a in (ident, dist, dist.T, rope, ids, far, rows)]


def kernel(L0_attn_x, L0_attn_qkv_w, L0_attn_proj_w, L0_attn_proj_b, L0_attn_slopes, L0_ffn_router_w, L0_ffn_w1,
           L0_ffn_v1, L0_ffn_w2, L0_ffn_bias):
    import concourse.bacc as bacc
    import numpy as np
    from concourse.bass_utils import run_bass_kernel_spmd

    qkv = np.asarray(L0_attn_qkv_w).reshape(3, H, HD, D)
    q, k = qkv[0].transpose(1, 0, 2), qkv[1].transpose(1, 0, 2)
    blocks = [q, k, np.roll(q, HD // 2, 0), np.roll(k, HD // 2, 0)]
    small = [b.reshape(P, D).T for b in blocks] + [qkv[2].reshape(P, D).T, np.asarray(L0_attn_proj_w).T,
                                                   np.asarray(L0_ffn_router_w)]
    ident, dist, dist_t, rope, ids, far, rows = _constants()
    arrays = {
        "x": L0_attn_x, "small_w": np.concatenate(small, 1), "w1": L0_ffn_w1, "v1": L0_ffn_v1, "w2": L0_ffn_w2,
        "ffn_bias": L0_ffn_bias, "proj_b": L0_attn_proj_b, "slopes": L0_attn_slopes, "ident": ident, "dist": dist,
        "dist_t": dist_t, "rope": rope, "expert_ids": ids, "far": far, "ones_rows": rows,
    }
    arrays = {"in_" + n: np.ascontiguousarray(a) for n, a in arrays.items()}
    nc = bacc.Bacc("TRN2", target_bir_lowering=False, num_devices=1)
    args = [nc.dram_tensor(n, a.shape, mybir.dt.from_np(a.dtype), kind="ExternalInput").ap() for n, a in arrays.items()]
    out = nc.dram_tensor("out", (B, N, D), F32, kind="ExternalOutput").ap()
    macaron(nc, *args, out)
    return run_bass_kernel_spmd(nc, [arrays], core_ids=[0]).results[0]["out"]
```

```python
from contextlib import ExitStack

import concourse.bass as bass
from concourse import mybir

F32 = mybir.dt.float32
F32R = mybir.dt.float32r
BF16 = mybir.dt.bfloat16
U32 = mybir.dt.uint32
ALU = mybir.AluOpType
ACT = mybir.ActivationFunctionType
AX = mybir.AxisListType

B, N, D = 8, 256, 128
P = 128
TB = N // P
H, HD = 16, 8
E, F = 8, 352
UNITS = E * TB
FT = E * F
CH = FT // P
EPS = 1e-5
VW = 32
PAIRS = [(0, 0), (1, 0), (2, 0), (0, 1), (1, 1), (0, 2)]
QK_ROWS = len(PAIRS) * HD
S_ROWS = QK_ROWS + 6
E_ROWS = S_ROWS + 2
ROUTE = 10
P2_AT = 5
LAG = 3
PASS_1 = {ch: (ch - 4) // 2 for ch in range(4, CH, 2)}
PASS_1_UP = {u: len(PASS_1) + u for u in range(16 - len(PASS_1))}
PASS_2 = {P2_AT + j * (CH - 1 - P2_AT) // 15: j for j in range(16)}


CQ, CK, CQR, CKR, CV, CP, CR, CEND = 0, 128, 256, 384, 512, 640, 768, 776


def macaron(nc, x, small_w, w1, v1, w2, ffn_bias, proj_b, slopes, ident, dist, dist_t, rope, expert_ids,
            far, ones_rows, out):
    ctx = ExitStack()
    with ctx:
        ctx.enter_context(nc.allow_low_precision(reason="exact splits"))

        def sb(name, shape, dt=F32):
            return ctx.enter_context(nc.sbuf_tensor(name, shape, dt))

        def sem(name):
            return ctx.enter_context(nc.semaphore(name))

        xres = sb("xres", [P, B * TB, D])
        wup_hi, wup_lo = sb("wup_hi", [D, E, 2 * F], F32R), sb("wup_lo", [D, E, 2 * F], F32R)
        wdn_hi, wdn_lo = sb("wdn_hi", [P, CH, D], F32R), sb("wdn_lo", [P, CH, D], F32R)
        wsm_hi, wsm_lo = sb("wsm_hi", [D, CEND], F32R), sb("wsm_lo", [D, CEND], F32R)
        stage = sb("stage", [P, E * 2 * F + CH * D])
        stage_up = stage[:, 0:E * 2 * F].rearrange("p (e f) -> p e f", e=E)
        stage_dn = stage[:, E * 2 * F:].rearrange("p (c d) -> p c d", c=CH)
        probs = stage[:, 0:TB * H * N].rearrange("p (k h n) -> p k h n", k=TB, h=H)
        idn = sb("idn", [P, P])
        near = sb("near", [P, H + 2, P])
        near_t = sb("near_t", [P, H, P])
        dist_sb, dist_t_sb = sb("dist_sb", [P, P]), sb("dist_t_sb", [P, P])
        slope_bc = sb("slope_bc", [P, H])
        rope_sb = sb("rope_sb", [P, 2, N])
        ids = sb("ids", [P, TB, E])
        half_bias = sb("half_bias", [D, 1])
        fbias = sb("fbias", [D, 1])
        pb_row = sb("pb_row", [1, D])
        one_row = sb("one_row", [1, P])
        mhalf = sb("mhalf", [P, TB])
        slope_col = sb("slope_col", [H, 1])
        hid = sb("hid", [P, TB, FT])
        stage_sm = hid[:, 0, 0:CEND]
        gel = sb("gel", [P, 2, F])
        hT_hi, hT_lo = sb("hT_hi", [P, 4, N], F32R), sb("hT_lo", [P, 4, N], F32R)
        yT = sb("yT", [D, N])
        bst = [sb(f"bst{w}", [P, TB, 6]) for w in range(3)]
        mv = [sb(f"mv{w}", [P, TB, 2]) for w in range(3)]
        veps = [sb(f"veps{w}", [P, TB]) for w in range(3)]
        rstd = [sb(f"rstd{w}", [P, TB]) for w in range(3)]
        xn = sb("xn", [P, TB, D])
        xT_hi = [sb(f"xT_hi{w}", [D, N], F32R) for w in range(3)]
        xT_lo = [sb(f"xT_lo{w}", [D, N], F32R) for w in range(3)]
        top = [sb(f"top{w}", [P, TB, 8]) for w in range(2)]
        ix = [sb(f"ix{w}", [P, TB, 8], U32) for w in range(2)]
        ixf = [sb(f"ixf{w}", [P, TB, 2]) for w in range(2)]
        nmx = [sb(f"nmx{w}", [P, TB]) for w in range(2)]
        ex = [sb(f"ex{w}", [P, TB, 8]) for w in range(2)]
        sm = [sb(f"sm{w}", [P, TB]) for w in range(2)]
        rs = [sb(f"rs{w}", [P, TB]) for w in range(2)]
        wts = [sb(f"wts{w}", [P, TB, 2]) for w in range(2)]
        eq = [sb(f"eq{w}", [P, 2, TB, E]) for w in range(2)]
        gw = [sb(f"gw{w}", [P, 2, TB, E]) for w in range(2)]
        gate = [sb(f"gate{w}", [P, TB, E]) for w in range(2)]
        rc = sb("rc", [P, 2, N])
        lev = sb("lev", [P, 3, 2, N], BF16)
        qs, ks = sb("qs", [E_ROWS, H, N], BF16), sb("ks", [E_ROWS, H, N], BF16)
        vaug = sb("vaug", [P, TB, H, VW])
        mx = sb("mx", [P, TB, H])
        nm = sb("nm", [P, TB, H])
        ml = sb("ml", [H, 2, N], BF16)
        oT = sb("oT", [P, 2 * N])
        rsn = oT[:, :].rearrange("p (s n) -> p s n", s=2)
        far_v, far_l = rsn[0:H], lev[0:H]
        rden = sb("rden", [P, 2, 4 * TB * 2, 1])
        att = xn
        aT_hi, aT_lo = xT_hi[1], xT_lo[1]

        d_lev = nc.dram_tensor("d_lev", (2, 3, P, N), BF16, kind="Internal").ap()
        d_far = nc.dram_tensor("d_far", (3, 2, H, N), BF16, kind="Internal").ap()
        d_max = nc.dram_tensor("d_max", (2, H, N), BF16, kind="Internal").ap()

        def pb(name):
            return ctx.enter_context(nc.psum_tensor(name, [P, 512], F32))

        psA, psV, psY = pb("psA"), pb("psV"), pb("psY")
        psA2, psV2 = pb("psA2"), pb("psV2")
        up_a, up_v = [psA, psA2], [psV, psV2]
        psT = [psA, psV, psA2, psV2]
        psS = [pb("psS0"), pb("psS1")]
        psM = pb("psM")

        score_banks = [*psS, psM]

        xin_landed, xrest_landed, small_landed, const_landed = (sem(n) for n in (
            "xin_landed", "xrest_landed", "small_landed", "const_landed"))
        up_landed = [sem(f"up_landed{e}") for e in range(E)]
        down_landed = sem("down_landed")
        wsm_hi_done, wsm_lo_done = sem("wsm_hi_done"), sem("wsm_lo_done")
        wup_hi_done, wup_lo_done = sem("wup_hi_done"), sem("wup_lo_done")
        wdn_hi_done, wdn_lo_done = sem("wdn_hi_done"), sem("wdn_lo_done")
        pool_const, near_done, far_val, far_step = sem("pool_const"), sem("near_done"), sem("far_val"), sem("far_step")
        far_out, rows_landed = sem("far_out"), sem("rows_landed")
        half_done = sem("half_done")
        a_full, v_full, gelu_done, hid_done = sem("a_full"), sem("v_full"), sem("gelu_done"), sem("hid_done")
        hT_full, hT_hi_done, hT_lo_done, down_done = sem("hT_full"), sem("hT_hi_done"), sem("hT_lo_done"), sem("down_done")
        yT_copied, y_full = sem("yT_copied"), sem("y_full")
        y_added, x2_done = sem("y_added"), sem("x2_done")
        LNS = ("f1", "at", "f2")
        stats_done = [sem(f"stats_done_{w}") for w in LNS]
        mean_done = [sem(f"mean_done_{w}") for w in LNS]
        eps_done = [sem(f"eps_done_{w}") for w in LNS]
        rstd_done = [sem(f"rstd_done_{w}") for w in LNS]
        xn_done = [sem(f"xn_done_{w}") for w in LNS]
        xT_full = [sem(f"xT_full_{w}") for w in LNS]
        xT_hi_done = [sem(f"xT_hi_done_{w}") for w in LNS]
        xT_lo_done = [sem(f"xT_lo_done_{w}") for w in LNS]
        logit_full = [sem(f"logit_full{w}") for w in range(2)]
        route = [sem(f"route{w}") for w in range(2)]
        nmx_done = [sem(f"nmx_done{w}") for w in range(2)]
        ex_done = [sem(f"ex_done{w}") for w in range(2)]
        gate_done = [sem(f"gate_done{w}") for w in range(2)]
        v_psum, v_copied = sem("v_psum"), sem("v_copied")
        qk_full, rot_full, cos_done, sin_done = sem("qk_full"), sem("rot_full"), sem("cos_done"), sem("sin_done")
        split_step, lev_out, stack_landed = sem("split_step"), sem("lev_out"), sem("stack_landed")
        s1_full, max_found = sem("s1_full"), sem("max_found")
        nm_done, mT_full, ml_hi, ml_done, ml_out, mrow_landed = (sem(n) for n in (
            "nm_done", "mT_full", "ml_hi", "ml_done", "ml_out", "mrow_landed"))
        s2_full, s2_biased, exp_done = sem("s2_full"), sem("s2_biased"), sem("exp_done")
        pv_full, oT_copied, o_full, rden_done, att_done = (sem(n) for n in (
            "pv_full", "oT_copied", "o_full", "rden_done", "att_done"))
        aT_full, aT_hi_done, aT_lo_done, proj_full = (sem(n) for n in ("aT_full", "aT_hi_done", "aT_lo_done", "proj_full"))
        stored = sem("stored")


        w1_v, v1_v = w1.rearrange("e d f -> d e f"), v1.rearrange("e d f -> d e f")
        w2_v = w2.rearrange("e f d -> (e f) d").rearrange("(c p) d -> p c d", p=P)
        out_v = out.rearrange("b (t p) d -> b p t d", p=P)
        block = ctx.enter_context(nc.Block())

        awaited = {}

        def const_first(eng, const_sem, const, by_batch_sem, value):
            if not isinstance(value, int):
                register = awaited.setdefault(eng, None) or eng.alloc_register("awaited")
                awaited[eng] = register
                eng.reg_mov(register, value)
                value = register
            eng.wait_ge(const_sem, const)
            eng.wait_ge(by_batch_sem, value)

        def iterations(eng, prologue, iteration):
            prologue()
            with eng.Fori(0, B - 3) as g:
                iteration(g, True, True, True)
            iteration(B - 3, True, True, False)
            iteration(B - 2, False, True, False)
            iteration(B - 1, False, False, False)

        def call_1(g):
            return g * 2 + 2

        def call_2(g, more):
            return g * 2 + 3 if more else B + g

        def first(c):
            return isinstance(c, int) and c == 0

        @block.sync
        def _(sp):
            sp.dma_start(xres[:, 0:TB, :], x[0].rearrange("(t p) d -> p t d", p=P)).then_inc(xin_landed, 16)
            sp.dma_start(stage_sm, small_w).then_inc(small_landed, 16)
            sp.dma_start(idn[:, :], ident).then_inc(const_landed, 16)
            sp.dma_start(ids[:, :, :], expert_ids).then_inc(const_landed, 16)
            for e in range(E):
                sp.dma_start(stage_up[:, e, 0:F], w1_v[:, e, :]).then_inc(up_landed[e], 16)
                sp.dma_start(stage_up[:, e, F:2 * F], v1_v[:, e, :]).then_inc(up_landed[e], 16)
            sp.dma_start(stage_dn, w2_v).then_inc(down_landed, 16)
            sp.dma_start(xres[:, TB:, :], x[1:].rearrange("b (t p) d -> p (b t) d", p=P)).then_inc(xrest_landed, 16)
            sp.wait_ge(far_step, 5)
            sp.dma_start(d_far.rearrange("l s h n -> h l s n"), far_l).then_inc(far_out, 16)
            sp.wait_ge(far_out, 16)
            sp.dma_start(ks[QK_ROWS:QK_ROWS + 3, :, :], d_far[:, 0]).then_inc(rows_landed, 16)
            sp.dma_start(qs[QK_ROWS + 3:S_ROWS, :, :], d_far[:, 1]).then_inc(rows_landed, 16)

            def stack(b):
                sp.wait_ge(split_step, b * 5 + 5)
                for s in range(2):
                    sp.dma_start(d_lev[s].rearrange("l p n -> p l n"), lev[:, :, s, :]).then_inc(lev_out, 16)
                sp.wait_ge(lev_out, b * 32 + 32)
                for s, dst in ((0, qs), (1, ks)):
                    for t, pair in enumerate(PAIRS):
                        sp.dma_start(dst[t * HD:(t + 1) * HD, :, :],
                                     d_lev[s, pair[s]].rearrange("(d h) n -> d h n", h=H)).then_inc(stack_landed, 16)

            def max_rows(b):
                sp.wait_ge(ml_done, b + 1)
                sp.dma_start(d_max.rearrange("l h n -> h l n"), ml[:, :, :]).then_inc(ml_out, 16)
                sp.wait_ge(ml_out, b * 16 + 16)
                sp.dma_start(qs[S_ROWS:E_ROWS, :, :], d_max).then_inc(mrow_landed, 16)

            def prologue():
                stack(0)
                max_rows(0)

            def iteration(g, more, nxt, ln0):
                if nxt:
                    stack(g + 1)
                    max_rows(g + 1)
                sp.wait_ge(y_added, call_2(g, more) + 1)
                sp.dma_start(out_v[g], xres[:, bass.ds(g * TB, TB), :]).then_inc(stored, 16)

            iterations(sp, prologue, iteration)
            sp.wait_ge(stored, B * 16)

        @block.gpsimd
        def _(pool):
            nc.gpsimd.memset(mhalf[:, :], -0.5)
            nc.gpsimd.memset(one_row[:, :], 1.0)
            nc.gpsimd.memset(near[:, :, :], 0.0)
            nc.gpsimd.memset(vaug[:, :, :, :], 0.0).then_inc(far_val, 1)
            pool.wait_ge(far_val, 1)
            nc.gpsimd.memset(vaug[:, :, :, HD:HD + 1], 1.0).then_inc(half_done, 1)
            pool.wait_ge(pool_const, 96)

            def rstd_of(w, b):
                const_first(pool, half_done, 1, mean_done[w], b * TB + TB)
                nc.gpsimd.tensor_scalar(veps[w][:, :], mv[w][:, :, 1], EPS, None, ALU.add).then_inc(eps_done[w], 1)
                pool.wait_ge(eps_done[w], b + 1)
                nc.gpsimd.tensor_tensor(rstd[w][:, :], veps[w][:, :], mhalf[:, :], ALU.pow).then_inc(rstd_done[w], 1)

            def split_qk(b):
                pool.wait_ge(cos_done, b + 1)
                pool.wait_ge(sin_done, b + 1)
                nc.gpsimd.tensor_tensor(rc[:, :, :], rc[:, :, :], rsn, ALU.add).then_inc(split_step, 1)
                pool.wait_ge(split_step, b * 5 + 2)
                nc.gpsimd.tensor_tensor(rc[:, :, :], rc[:, :, :], lev[:, 0], ALU.subtract).then_inc(split_step, 1)
                pool.wait_ge(split_step, b * 5 + 4)
                nc.gpsimd.tensor_tensor(lev[:, 2], rc[:, :, :], lev[:, 1], ALU.subtract).then_inc(split_step, 1)

            def prologue():
                rstd_of(0, 0)
                nc.gpsimd.tensor_scalar(half_bias[:, :], fbias[:, :], 0.5, None, ALU.mult).then_inc(half_done, 1)
                rstd_of(0, 1)
                for h in range(H):
                    nc.gpsimd.tensor_scalar(near[:, h + 1, :], dist_sb[:, :], slope_bc[:, h:h + 1], 8.0,
                                            ALU.mult, ALU.mult).then_inc(near_done, 1)
                    nc.gpsimd.tensor_scalar(near_t[:, h, :], dist_t_sb[:, :], slope_bc[:, h:h + 1], 8.0,
                                            ALU.mult, ALU.mult).then_inc(near_done, 1)
                nc.gpsimd.tensor_scalar(far_v, far_v, slope_col[:, :], 8.0, ALU.mult, ALU.mult).then_inc(far_step, 1)
                pool.wait_ge(far_step, 1)
                nc.gpsimd.tensor_copy(far_l[:, 0], far_v).then_inc(far_step, 1)
                pool.wait_ge(far_step, 2)
                nc.gpsimd.tensor_tensor(far_v, far_v, far_l[:, 0], ALU.subtract).then_inc(far_step, 1)
                pool.wait_ge(far_step, 3)
                nc.gpsimd.tensor_copy(far_l[:, 1], far_v).then_inc(far_step, 1)
                pool.wait_ge(far_step, 4)
                nc.gpsimd.tensor_tensor(far_l[:, 2], far_v, far_l[:, 1], ALU.subtract).then_inc(far_step, 1)
                pool.wait_ge(far_out, 16)
                rstd_of(1, 0)
                rstd_of(0, 2)
                split_qk(0)

            def iteration(g, more, nxt, ln0):
                if nxt:
                    rstd_of(1, g + 1)
                    split_qk(g + 1)
                rstd_of(2, g)
                if ln0:
                    rstd_of(0, g + 3)

            iterations(pool, prologue, iteration)

        @block.scalar
        def _(act):
            act.dma_start(slope_bc[:, :], slopes.partition_broadcast(P)).then_inc(pool_const, 16)
            act.dma_start(dist_sb[:, :], dist).then_inc(pool_const, 16)
            act.dma_start(dist_t_sb[:, :], dist_t).then_inc(pool_const, 16)
            act.dma_start(fbias[:, :], ffn_bias.rearrange("(d o) -> d o", o=1)).then_inc(pool_const, 16)
            act.dma_start(slope_col[:, :], slopes.rearrange("(h o) -> h o", o=1)).then_inc(pool_const, 16)
            act.dma_start(far_v, far).then_inc(pool_const, 16)
            act.dma_start(rope_sb[:, :, :], rope).then_inc(const_landed, 16)
            act.dma_start(pb_row[:, :], proj_b.rearrange("(o d) -> o d", o=1)).then_inc(const_landed, 16)
            act.dma_start(qs[QK_ROWS:QK_ROWS + 3, :, :], ones_rows[0:3]).then_inc(rows_landed, 16)
            act.dma_start(ks[QK_ROWS + 3:E_ROWS, :, :], ones_rows[3:8]).then_inc(rows_landed, 16)
            copy, gelu, exp, ident_f = ACT.Copy, ACT.Gelu, ACT.Exp, ACT.Identity

            def xT_high(w, b):
                act.wait_ge(xT_full[w], b + 1)
                nc.scalar.activation(xT_hi[w][:, :], psM[:, 0:N], copy).then_inc(xT_hi_done[w], 1)

            def router_exp(r, b):
                act.wait_ge(nmx_done[r], b + 1)
                for t in range(TB):
                    nc.scalar.activation(ex[r][:, t, :], top[r][:, t, :], exp, bias=nmx[r][:, t:t + 1],
                                         accum_out=sm[r][:, t:t + 1]).then_inc(ex_done[r], 1)

            def gate_gelu(c, u):
                act.wait_ge(a_full, c * UNITS + (u + 1))
                if u >= 2 or not first(c):
                    act.wait_ge(hid_done, c * UNITS + (u - 1))
                nc.scalar.activation(gel[:, u % 2, :], up_a[u % 2][:, 0:F], gelu).then_inc(gelu_done, 1)

            def hid_high(c, ch):
                act.wait_ge(hT_full, c * CH + (ch + 1))
                if ch == 0 and not first(c):
                    act.wait_ge(down_done, c * CH)
                if ch >= 4:
                    act.wait_ge(down_done, c * CH + (ch - 3))
                nc.scalar.activation(hT_hi[:, ch % 4, :], psT[ch % 4][:, 0:N], copy).then_inc(hT_hi_done, 1)

            def y_copy(c):
                act.wait_ge(down_done, c * CH + CH)
                nc.scalar.activation(yT[:, :], psY[:, 0:N], ident_f, bias=half_bias[:, 0:1]).then_inc(yT_copied, 1)

            def values(b):
                act.wait_ge(v_psum, b + 1)
                nc.scalar.activation(vaug[:, :, :, 0:HD],
                                     psM[:, N:2 * N].rearrange("p (t h d) -> p t h d", t=TB, h=H), copy).then_inc(v_copied, 1)

            def part(b, level):
                act.wait_ge(split_step, b * 5 + (2 * level + 1))
                nc.scalar.activation(lev[:, level], rc[:, :, :], copy).then_inc(split_step, 1)

            def max_high(b):
                act.wait_ge(mT_full, b + 1)
                nc.scalar.activation(ml[:, 0, :], psM[0:H, 0:N], copy).then_inc(ml_hi, 1)

            def attention_exp(b, j):
                act.wait_ge(s2_biased, b * 16 + (j + 1))
                hp, kt = j // 2, j % 2
                nc.scalar.activation(probs[:, kt, 2 * hp:2 * hp + 2, :],
                                     score_banks[j % 3][:, :].rearrange("p (h n) -> p h n", h=2), exp).then_inc(exp_done, 1)

            def oT_copy(b, half, split=0):
                act.wait_ge(pv_full, b * 2 + (half + 1))
                if half == 0 and split:
                    act.wait_ge(split_step, b * 5 + 6)
                nc.scalar.activation(oT[:, :], psM[:, :], copy).then_inc(oT_copied, 1)

            def aT_high(b):
                act.wait_ge(aT_full, b + 1)
                nc.scalar.activation(aT_hi[:, :], psM[:, 0:N], copy).then_inc(aT_hi_done, 1)

            def prologue():
                act.wait_ge(small_landed, 16)
                nc.scalar.activation(wsm_hi[:, :], stage_sm, copy).then_inc(wsm_hi_done, 1)
                xT_high(0, 0)
                router_exp(0, 0)
                for e in range(E):
                    act.wait_ge(up_landed[e], 32)
                    nc.scalar.activation(wup_hi[:, e, :], stage_up[:, e, :], copy).then_inc(wup_hi_done, 1)
                    for u in (2 * e, 2 * e + 1):
                        gate_gelu(0, u)
                act.wait_ge(down_landed, 16)
                nc.scalar.activation(wdn_hi[:, :, :], stage_dn, copy).then_inc(wdn_hi_done, 1)
                act.wait_ge(half_done, 2)
                for ch in range(CH):
                    hid_high(0, ch)
                    if ch == 4:
                        xT_high(0, 1)
                    if ch == 8:
                        router_exp(0, 1)
                y_copy(0)
                for u in range(UNITS):
                    gate_gelu(1, u)
                    if u == 4:
                        xT_high(1, 0)
                    if u == 6:
                        values(0)
                    if u == 12:
                        act.wait_ge(far_out, 16)
                        part(0, 0)
                    if u == 14:
                        part(0, 1)
                for ch in range(CH):
                    hid_high(1, ch)
                    if ch == 3:
                        xT_high(0, 2)
                    if ch == 8:
                        router_exp(0, 2)
                y_copy(1)
                max_high(0)
                for j in range(16):
                    attention_exp(0, j)

            def iteration(g, more, nxt, ln0):
                c1, c2 = call_1(g), call_2(g, more)
                for u in range(UNITS):
                    if more:
                        gate_gelu(c1, u)
                    if nxt and u == 2:
                        xT_high(1, g + 1)
                    if u == 7:
                        oT_copy(g, 0, split=nxt)
                    if nxt and u == 8:
                        part(g + 1, 0)
                    if nxt and u == 10:
                        part(g + 1, 1)
                    if u == 11:
                        oT_copy(g, 1)
                    if nxt and u == 15:
                        values(g + 1)
                for ch in range(CH):
                    if more:
                        hid_high(c1, ch)
                    if ch == 1:
                        aT_high(g)
                    if ch == 9:
                        xT_high(2, g)
                    if ch == 14:
                        router_exp(1, g)
                if more:
                    y_copy(c1)
                for u in range(UNITS):
                    gate_gelu(c2, u)
                    if nxt and u == 9:
                        max_high(g + 1)
                    if ln0 and u == 11:
                        xT_high(0, g + 3)
                    if ln0 and u == 15:
                        router_exp(0, g + 3)
                for ch in range(CH):
                    hid_high(c2, ch)
                    if nxt and ch - 1 in PASS_2:
                        attention_exp(g + 1, PASS_2[ch - 1])
                if nxt:
                    attention_exp(g + 1, 15)
                y_copy(c2)

            iterations(act, prologue, iteration)

        @block.vector
        def _(dve):
            def ln_stats(w, b):
                for t in range(TB):
                    nc.vector.bn_stats(bst[w][:, t, :], xres[:, b * TB + t, :]).then_inc(stats_done[w], 1)
                for t in range(TB):
                    const_first(dve, xin_landed, 16, stats_done[w], b * TB + (t + 1))
                    nc.vector.bn_aggr(mv[w][:, t, :], bst[w][:, t, :]).then_inc(mean_done[w], 1)

            def ln_apply(w, b):
                dve.wait_ge(rstd_done[w], b + 1)
                for t in range(TB):
                    nc.vector.tensor_scalar(xn[:, t, :], xres[:, b * TB + t, :], mv[w][:, t, 0:1], rstd[w][:, t:t + 1],
                                            ALU.subtract, ALU.mult).then_inc(xn_done[w], 1)

            def xT_low(w, b):
                dve.wait_ge(xT_hi_done[w], b + 1)
                nc.vector.tensor_tensor(xT_lo[w][:, :], psM[:, 0:N], xT_hi[w][:, :].bitcast(F32), ALU.subtract).then_inc(
                    xT_lo_done[w], 1)

            def route_top(r, b):
                const_first(dve, const_landed, 64, logit_full[r], b + 1)
                for t in range(TB):
                    nc.vector.max(top[r][:, t, :], psM[:, N + 8 * t:N + 8 * t + 8]).then_inc(route[r], 1)
                dve.wait_ge(route[r], b * ROUTE + 2)
                nc.vector.tensor_scalar(nmx[r][:, :], top[r][:, :, 0], -1.0, None, ALU.mult).then_inc(nmx_done[r], 1)
                for t in range(TB):
                    nc.vector.max_index(ix[r][:, t, :], top[r][:, t, :], psM[:, N + 8 * t:N + 8 * t + 8]).then_inc(route[r], 1)
                dve.wait_ge(route[r], b * ROUTE + 4)
                nc.vector.tensor_copy(ixf[r][:, :, :], ix[r][:, :, 0:2]).then_inc(route[r], 1)

            def route_gate(r, b):
                dve.wait_ge(route[r], b * ROUTE + 5)
                nc.vector.tensor_tensor(eq[r][:, :, :, :], ids[:, None, :, :].broadcast_to([P, 2, TB, E]),
                                        ixf[r][:, :, :].rearrange("p t k -> p k t")[:, :, :, None].broadcast_to([P, 2, TB, E]),
                                        ALU.is_equal).then_inc(route[r], 1)
                dve.wait_ge(ex_done[r], b * TB + TB)
                nc.vector.tensor_scalar(sm[r][:, :], sm[r][:, :], 2.0, None, ALU.mult).then_inc(route[r], 1)
                dve.wait_ge(route[r], b * ROUTE + 7)
                nc.vector.reciprocal(rs[r][:, :], sm[r][:, :]).then_inc(route[r], 1)
                dve.wait_ge(route[r], b * ROUTE + 8)
                nc.vector.tensor_tensor(wts[r][:, :, :], ex[r][:, :, 0:2], rs[r][:, :, None].broadcast_to([P, TB, 2]),
                                        ALU.mult).then_inc(route[r], 1)
                dve.wait_ge(route[r], b * ROUTE + 9)
                nc.vector.tensor_tensor(gw[r][:, :, :, :], eq[r][:, :, :, :],
                                        wts[r][:, :, :].rearrange("p t k -> p k t")[:, :, :, None].broadcast_to([P, 2, TB, E]),
                                        ALU.mult).then_inc(route[r], 1)
                dve.wait_ge(route[r], b * ROUTE + 10)
                nc.vector.tensor_tensor(gate[r][:, :, :], gw[r][:, 0], gw[r][:, 1], ALU.add).then_inc(gate_done[r], 1)

            def gated(r, b, c, u):
                e, t = u // TB, u % TB
                if u == 0:
                    dve.wait_ge(gate_done[r], b + 1)
                    if not first(c):
                        dve.wait_ge(hT_full, c * CH)
                dve.wait_ge(gelu_done, c * UNITS + (u + 1))
                dve.wait_ge(v_full, c * UNITS + (u + 1))
                nc.vector.scalar_tensor_tensor(out=hid[:, t, e * F:(e + 1) * F], in0=up_v[u % 2][:, 0:F],
                                               scalar=gate[r][:, t, e:e + 1], in1=gel[:, u % 2, :],
                                               op0=ALU.mult, op1=ALU.mult).then_inc(hid_done, 1)

            def hid_low(c, ch):
                dve.wait_ge(hT_hi_done, c * CH + (ch + 1))
                nc.vector.tensor_tensor(hT_lo[:, ch % 4, :], psT[ch % 4][:, 0:N], hT_hi[:, ch % 4, :].bitcast(F32), ALU.subtract
                                        ).then_inc(hT_lo_done, 1)

            def y_add(c, b):
                dve.wait_ge(y_full, c + 1)
                nc.vector.tensor_tensor(xres[:, bass.ds(b * TB, TB), :], xres[:, bass.ds(b * TB, TB), :],
                                        psY[:, N:2 * N].rearrange("p (t d) -> p t d", t=TB), ALU.add).then_inc(y_added, 1)

            def rotate(b):
                dve.wait_ge(qk_full, b + 1)
                if not (isinstance(b, int) and b == 0):
                    dve.wait_ge(split_step, b * 5)
                nc.vector.tensor_tensor(rc[:, :, :], psM[:, :].rearrange("p (s n) -> p s n", s=2), rope_sb[:, 0:1, :].broadcast_to([P, 2, N]), ALU.mult
                                        ).then_inc(cos_done, 1)

            def rotate_2(b):
                dve.wait_ge(rot_full, b + 1)
                nc.vector.tensor_tensor(rsn, psM[:, :].rearrange("p (s n) -> p s n", s=2), rope_sb[:, 1:2, :].broadcast_to([P, 2, N]), ALU.mult
                                        ).then_inc(sin_done, 1)

            def row_max(b, i):
                qt, hp = i // 8, i % 8
                const_first(dve, near_done, 2 * H, s1_full, b * 16 + (i + 1))
                for j in range(2):
                    h = 2 * hp + j
                    bias = near[:, h + 1:H + 2:H - h, :] if qt == 0 else near[:, 0:h + 2:h + 1, :]
                    part = psS[i % 2][:, j * N:(j + 1) * N].rearrange("p (a n) -> p a n", a=TB)
                    nc.vector.tensor_tensor_reduce(out=part, in0=part, in1=bias,
                                                   scale=1.0, scalar=-3.0e38, op0=ALU.add, op1=ALU.max,
                                                   accum_out=mx[:, qt, h:h + 1]).then_inc(max_found, 1)

            def max_negate(b):
                dve.wait_ge(max_found, b * 32 + 32)
                nc.vector.tensor_scalar(nm[:, :, :], mx[:, :, :], -1.0, None, ALU.mult).then_inc(nm_done, 1)

            def max_low(b):
                dve.wait_ge(ml_hi, b + 1)
                nc.vector.tensor_tensor(ml[:, 1, :], psM[0:H, 0:N], ml[:, 0, :], ALU.subtract).then_inc(ml_done, 1)

            def near_bias(b, j):
                hp, kt = j // 2, j % 2
                dve.wait_ge(s2_full, b * 16 + (j + 1))
                part = score_banks[j % 3][:, :].rearrange("p (h n) -> p h n", h=2)[:, :, kt * P:(kt + 1) * P]
                nc.vector.tensor_tensor(part, part, near_t[:, 2 * hp:2 * hp + 2, :], ALU.add).then_inc(s2_biased, 1)

            def normalize(b, half):
                dve.wait_ge(o_full, b * 2 + (half + 1))
                nc.vector.reciprocal(rden[:, half], psM[:, :].rearrange("p (x v) -> p x v", v=VW)[:, :, HD:HD + 1]
                                     ).then_inc(rden_done, 1)
                dve.wait_ge(rden_done, b * 2 + (half + 1))
                for qt in range(TB):
                    o = psM[:, :].rearrange("p (a q j v) -> p a q j v", a=2, q=TB, j=4)[:, :, qt, :, 0:HD]
                    r = rden[:, half].rearrange("p (a q j) o -> p a q j o", a=2, q=TB)[:, :, qt, :, :].broadcast_to([P, 2, 4, HD])
                    nc.vector.tensor_tensor(att[:, qt, half * 64:(half + 1) * 64].rearrange("p (a j d) -> p a j d", a=2, j=4),
                                            o, r, ALU.mult).then_inc(att_done, 1)

            def aT_low(b):
                dve.wait_ge(aT_hi_done, b + 1)
                nc.vector.tensor_tensor(aT_lo[:, :], psM[:, 0:N], aT_hi[:, :].bitcast(F32), ALU.subtract).then_inc(aT_lo_done, 1)

            def attention_add(b):
                dve.wait_ge(proj_full, b + 1)
                nc.vector.tensor_tensor(xres[:, bass.ds(b * TB, TB), :], xres[:, bass.ds(b * TB, TB), :],
                                        psM[:, 0:N].rearrange("p (t d) -> p t d", t=TB), ALU.add).then_inc(x2_done, 1)

            def prologue():
                dve.wait_ge(xin_landed, 16)
                ln_stats(0, 0)
                ln_apply(0, 0)
                dve.wait_ge(wsm_hi_done, 1)
                nc.vector.tensor_tensor(wsm_lo[:, :], stage_sm, wsm_hi[:, :].bitcast(F32), ALU.subtract).then_inc(wsm_lo_done, 1)
                xT_low(0, 0)
                route_top(0, 0)
                route_gate(0, 0)
                for e in range(E):
                    dve.wait_ge(wup_hi_done, e + 1)
                    nc.vector.tensor_tensor(wup_lo[:, e, :], stage_up[:, e, :], wup_hi[:, e, :].bitcast(F32), ALU.subtract
                                            ).then_inc(wup_lo_done, 1)
                    for u in (2 * e, 2 * e + 1):
                        gated(0, 0, 0, u)
                dve.wait_ge(xrest_landed, 16)
                ln_stats(0, 1)
                dve.wait_ge(wdn_hi_done, 1)
                nc.vector.tensor_tensor(wdn_lo[:, :, :], stage_dn, wdn_hi[:, :, :].bitcast(F32), ALU.subtract).then_inc(wdn_lo_done, 1)
                ln_apply(0, 1)
                for ch in range(CH):
                    hid_low(0, ch)
                    if ch == 4:
                        xT_low(0, 1)
                    if ch == 7:
                        route_top(0, 1)
                    if ch == 10:
                        route_gate(0, 1)
                y_add(0, 0)
                for u in range(UNITS):
                    gated(0, 1, 1, u)
                    if u == 0:
                        dve.wait_ge(y_added, 1)
                        ln_stats(1, 0)
                    if u == 2:
                        ln_apply(1, 0)
                    if u == 4:
                        xT_low(1, 0)
                    if u == 5:
                        ln_stats(0, 2)
                    if u == 7:
                        rotate(0)
                    if u == 9:
                        dve.wait_ge(far_step, 5)
                        rotate_2(0)
                    if u == 15:
                        ln_apply(0, 2)
                for ch in range(CH):
                    hid_low(1, ch)
                    if ch == 3:
                        xT_low(0, 2)
                    if ch == 6:
                        route_top(0, 2)
                    if ch == 10:
                        route_gate(0, 2)
                    if ch >= 8:
                        row_max(0, ch - 8)
                y_add(1, 1)
                for i in range(CH - 8, 16):
                    row_max(0, i)
                max_negate(0)
                max_low(0)
                for j in range(16):
                    near_bias(0, j)

            def iteration(g, more, nxt, ln0):
                c1, c2 = call_1(g), call_2(g, more)
                for u in range(UNITS):
                    if nxt and u == 0:
                        const_first(dve, xin_landed, 16, y_added, g * 2 + 2)
                        ln_stats(1, g + 1)
                    if more:
                        gated(0, g + 2, c1, u)
                    if nxt and u == 0:
                        ln_apply(1, g + 1)
                    if nxt and u == 2:
                        xT_low(1, g + 1)
                    if nxt and u == 4:
                        rotate(g + 1)
                    if nxt and u == 6:
                        rotate_2(g + 1)
                    if u == 9:
                        normalize(g, 0)
                    if u == 13:
                        normalize(g, 1)
                for ch in range(CH):
                    if more:
                        hid_low(c1, ch)
                    if ch == 1:
                        aT_low(g)
                    if ch == 4:
                        attention_add(g)
                        const_first(dve, xin_landed, 16, x2_done, g + 1)
                        ln_stats(2, g)
                    if ch == 6:
                        ln_apply(2, g)
                    if ch == 9:
                        xT_low(2, g)
                    if ch == 12:
                        route_top(1, g)
                    if ch == 17:
                        route_gate(1, g)
                    if nxt and ch in PASS_1:
                        row_max(g + 1, PASS_1[ch])
                if more:
                    y_add(c1, g + 2)
                for u in range(UNITS):
                    gated(1, g, c2, u)
                    if nxt and u in PASS_1_UP:
                        row_max(g + 1, PASS_1_UP[u])
                    if nxt and u == 8:
                        max_negate(g + 1)
                    if ln0 and u == 8:
                        ln_stats(0, g + 3)
                    if nxt and u == 9:
                        max_low(g + 1)
                    if ln0 and u == 10:
                        ln_apply(0, g + 3)
                    if ln0 and u == 11:
                        xT_low(0, g + 3)
                    if ln0 and u == 13:
                        route_top(0, g + 3)
                for ch in range(CH):
                    hid_low(c2, ch)
                    if ln0 and ch == 1:
                        route_gate(0, g + 3)
                    if nxt and ch in PASS_2:
                        near_bias(g + 1, PASS_2[ch])
                y_add(c2, g)

            iterations(dve, prologue, iteration)

        @block.tensor
        def _(pe):
            def mm3(o, l_hi, l_lo, r_hi, r_lo, start=True, stop=True):
                nc.tensor.matmul(o, l_hi, r_hi, start=start, stop=False)
                nc.tensor.matmul(o, l_hi, r_lo, start=False, stop=False)
                return nc.tensor.matmul(o, l_lo, r_hi, start=False, stop=stop)

            def ln_T(w, b):
                pe.wait_ge(xn_done[w], b * TB + TB)
                for t in range(TB):
                    i = nc.tensor.transpose(psM[:, t * P:(t + 1) * P], xn[:, t, :], idn[:, :])
                i.then_inc(xT_full[w], 1)

            def logits(r, b):
                w = 2 * r
                pe.wait_ge(xT_lo_done[w], b + 1)
                for t in range(TB):
                    s = slice(t * P, (t + 1) * P)
                    i = mm3(psM[:, N + 8 * t:N + 8 * t + 8], xT_hi[w][:, s], xT_lo[w][:, s], wsm_hi[:, CR:CEND], wsm_lo[:, CR:CEND])
                i.then_inc(logit_full[r], 1)

            def up_gate(r, c, u):
                e, t, w = u // TB, u % TB, 2 * r
                if u >= 2 or (u == 0 and not first(c)):
                    pe.wait_ge(gelu_done, c * UNITS + (u - 1))
                s = slice(t * P, (t + 1) * P)
                mm3(up_a[u % 2][:, 0:F], xT_hi[w][:, s], xT_lo[w][:, s], wup_hi[:, e, 0:F], wup_lo[:, e, 0:F]).then_inc(a_full, 1)

            def up_value(r, c, u):
                e, t, w = u // TB, u % TB, 2 * r
                if u >= 2 or (u == 0 and not first(c)):
                    pe.wait_ge(hid_done, c * UNITS + (u - 1))
                s = slice(t * P, (t + 1) * P)
                mm3(up_v[u % 2][:, 0:F], xT_hi[w][:, s], xT_lo[w][:, s], wup_hi[:, e, F:2 * F], wup_lo[:, e, F:2 * F]).then_inc(v_full, 1)

            def down_T(c, ch):
                if ch in (0, 2):
                    pe.wait_ge(hid_done, c * UNITS + (UNITS - 1 + ch // 2))
                if ch >= 4:
                    pe.wait_ge(hT_lo_done, c * CH + (ch - 3))
                for t in range(TB):
                    i = nc.tensor.transpose(psT[ch % 4][:, t * P:(t + 1) * P], hid[:, t, ch * P:(ch + 1) * P], idn[:, :])
                i.then_inc(hT_full, 1)

            def down_mm(c, ch):
                pe.wait_ge(hT_lo_done, c * CH + (ch + 1))
                if ch == 0 and not first(c):
                    pe.wait_ge(y_added, c)
                r_hi, r_lo = hT_hi[:, ch % 4, :], hT_lo[:, ch % 4, :]
                nc.tensor.matmul(psY[:, 0:N], wdn_hi[:, ch, :], r_hi, start=(ch == 0), stop=False)
                nc.tensor.matmul(psY[:, 0:N], wdn_hi[:, ch, :], r_lo, start=False, stop=False)
                nc.tensor.matmul(psY[:, 0:N], wdn_lo[:, ch, :], r_hi, start=False, stop=(ch == CH - 1)).then_inc(down_done, 1)

            def down_end(c):
                for ch in range(CH - LAG, CH):
                    down_mm(c, ch)
                y_T(c)

            def y_T(c):
                pe.wait_ge(yT_copied, c + 1)
                for t in range(TB):
                    i = nc.tensor.transpose(psY[:, N + t * P:N + (t + 1) * P], yT[:, t * P:(t + 1) * P], idn[:, :])
                i.then_inc(y_full, 1)

            def value_mm(b):
                pe.wait_ge(xT_lo_done[1], b + 1)
                for t in range(TB):
                    s = slice(t * P, (t + 1) * P)
                    i = mm3(psM[:, N + t * P:N + (t + 1) * P], xT_hi[1][:, s], xT_lo[1][:, s],
                            wsm_hi[:, CV:CV + P], wsm_lo[:, CV:CV + P])
                i.then_inc(v_psum, 1)

            def qk_mm(first, full):
                for s in range(2):
                    c = slice(first + s * P, first + (s + 1) * P)
                    i = mm3(psM[:, s * N:(s + 1) * N], wsm_hi[:, c], wsm_lo[:, c], xT_hi[1][:, :], xT_lo[1][:, :])
                i.then_inc(full, 1)

            def qk(b):
                pe.wait_ge(xT_lo_done[1], b + 1)
                qk_mm(CQ, qk_full)

            def rot(b):
                pe.wait_ge(cos_done, b + 1)
                qk_mm(CQR, rot_full)

            def scores_1(b, i):
                qt, hp = i // 8, i % 8
                if i == 0:
                    pe.wait_ge(stack_landed, b * (16 * 2 * len(PAIRS)) + 16 * 2 * len(PAIRS))
                    if not (isinstance(b, int) and b == 0):
                        pe.wait_ge(exp_done, b * 16)
                if i >= 2:
                    pe.wait_ge(max_found, b * 32 + 2 * (i - 1))
                for j in range(2):
                    h = 2 * hp + j
                    m = nc.tensor.matmul(psS[i % 2][:, j * N:(j + 1) * N], qs[0:S_ROWS, h, qt * P:(qt + 1) * P],
                                         ks[0:S_ROWS, h, :], start=True, stop=True)
                m.then_inc(s1_full, 1)

            def max_T(b):
                pe.wait_ge(nm_done, b + 1)
                if isinstance(b, int) and b == 0:
                    pe.wait_ge(route[0], 2 * ROUTE + 4)
                else:
                    pe.wait_ge(route[1], (b - 1) * ROUTE + 4)
                for t in range(TB):
                    i = nc.tensor.transpose(psM[0:H, t * P:(t + 1) * P], nm[:, t, :], idn[:, :])
                i.then_inc(mT_full, 1)

            def scores_2(b, j, ln0=False):
                hp, kt = j // 2, j % 2
                if j == 0:
                    pe.wait_ge(mrow_landed, b * 16 + 16)
                    pe.wait_ge(max_found, b * 32 + 32)
                if j == 2 and ln0:
                    pe.wait_ge(route[0], (b + 2) * ROUTE + 4)
                if j >= 3:
                    pe.wait_ge(exp_done, b * 16 + (j - 2))
                for a in range(2):
                    h = 2 * hp + a
                    m = nc.tensor.matmul(score_banks[j % 3][:, a * N:(a + 1) * N], ks[0:E_ROWS, h, kt * P:(kt + 1) * P],
                                         qs[0:E_ROWS, h, :], start=True, stop=True)
                m.then_inc(s2_full, 1)

            def weighted_values(b, half):
                pe.wait_ge(exp_done, b * 16 + 8 * (half + 1))
                if half:
                    pe.wait_ge(att_done, b * 4 + 2)
                for a in range(2):
                    for kt in range(TB):
                        for j in range(4):
                            h = half * 8 + a * 4 + j
                            m = nc.tensor.matmul(psM[j * VW:(j + 1) * VW, a * N:(a + 1) * N], vaug[:, kt, h, :],
                                                 probs[:, kt, h, :], start=(kt == 0), stop=(kt == TB - 1),
                                                 tile_position=(0, j * VW))
                m.then_inc(pv_full, 1)

            def out_T(b, half):
                pe.wait_ge(oT_copied, b * 2 + (half + 1))
                for x4 in range(4):
                    m = nc.tensor.transpose(psM[:, x4 * P:(x4 + 1) * P], oT[:, x4 * P:(x4 + 1) * P], idn[:, :])
                m.then_inc(o_full, 1)

            def att_T(b):
                pe.wait_ge(att_done, b * 4 + 4)
                for t in range(TB):
                    m = nc.tensor.transpose(psM[:, t * P:(t + 1) * P], att[:, t, :], idn[:, :])
                m.then_inc(aT_full, 1)

            def project(b):
                pe.wait_ge(aT_lo_done, b + 1)
                for t in range(TB):
                    s, o = slice(t * P, (t + 1) * P), psM[:, t * P:(t + 1) * P]
                    mm3(o, aT_hi[:, s], aT_lo[:, s], wsm_hi[:, CP:CP + P], wsm_lo[:, CP:CP + P], stop=False)
                    m = nc.tensor.matmul(o, one_row[:, :], pb_row[:, :], start=False, stop=True)
                m.then_inc(proj_full, 1)

            def prologue():
                pe.wait_ge(const_landed, 64)
                ln_T(0, 0)
                pe.wait_ge(wsm_lo_done, 1)
                logits(0, 0)
                for u in range(UNITS):
                    if u % TB == 0:
                        pe.wait_ge(wup_lo_done, u // TB + 1)
                    up_gate(0, 0, u)
                    up_value(0, 0, u)
                pe.wait_ge(wdn_lo_done, 1)
                for ch in range(CH):
                    down_T(0, ch)
                    if ch == 4:
                        pe.wait_ge(gate_done[0], 1)
                        ln_T(0, 1)
                    if ch == 7:
                        logits(0, 1)
                    if ch >= LAG:
                        down_mm(0, ch - LAG)
                down_end(0)
                for u in range(UNITS):
                    up_gate(0, 1, u)
                    if u == 4:
                        pe.wait_ge(gate_done[0], 2)
                        ln_T(1, 0)
                    if u == 6:
                        value_mm(0)
                    if u == 7:
                        pe.wait_ge(v_copied, 1)
                        qk(0)
                    if u == 8:
                        rot(0)
                    up_value(0, 1, u)
                for ch in range(CH):
                    down_T(1, ch)
                    if ch == 3:
                        pe.wait_ge(sin_done, 1)
                        ln_T(0, 2)
                    if ch == 6:
                        logits(0, 2)
                    if ch == 8:
                        pe.wait_ge(rows_landed, 64)
                    if ch >= 8:
                        scores_1(0, ch - 8)
                    if ch >= LAG:
                        down_mm(1, ch - LAG)
                down_end(1)
                for i in range(CH - 8, 16):
                    scores_1(0, i)
                max_T(0)
                for j in range(16):
                    scores_2(0, j)

            def iteration(g, more, nxt, ln0):
                c1, c2 = call_1(g), call_2(g, more)
                for u in range(UNITS):
                    if more:
                        up_gate(0, c1, u)
                    if nxt and u == 2:
                        pe.wait_ge(exp_done, g * 16 + 16)
                        ln_T(1, g + 1)
                    if nxt and u == 3:
                        qk(g + 1)
                    if nxt and u == 5:
                        rot(g + 1)
                    if u == 7:
                        if nxt:
                            pe.wait_ge(sin_done, g + 2)
                        else:
                            pe.wait_ge(exp_done, g * 16 + 16)
                        weighted_values(g, 0)
                    if u == 9:
                        out_T(g, 0)
                    if u == 11:
                        weighted_values(g, 1)
                    if u == 13:
                        out_T(g, 1)
                    if nxt and u == 15:
                        pe.wait_ge(att_done, g * 4 + 4)
                        value_mm(g + 1)
                    if more:
                        up_value(0, c1, u)
                for ch in range(CH):
                    if more:
                        down_T(c1, ch)
                    if ch == 1:
                        if nxt:
                            pe.wait_ge(v_copied, g + 2)
                        att_T(g)
                    if ch == 3:
                        project(g)
                    if ch == 9:
                        pe.wait_ge(x2_done, g + 1)
                        ln_T(2, g)
                    if ch == 12:
                        logits(1, g)
                    if nxt and ch in PASS_1:
                        scores_1(g + 1, PASS_1[ch])
                    if more and ch >= LAG:
                        down_mm(c1, ch - LAG)
                if more:
                    down_end(c1)
                for u in range(UNITS):
                    up_gate(1, c2, u)
                    if nxt and u in PASS_1_UP:
                        scores_1(g + 1, PASS_1_UP[u])
                    if nxt and u == 9:
                        max_T(g + 1)
                    if ln0 and u == 11:
                        pe.wait_ge(ml_done, g + 2)
                        ln_T(0, g + 3)
                    if ln0 and u == 13:
                        logits(0, g + 3)
                    up_value(1, c2, u)
                for ch in range(CH):
                    down_T(c2, ch)
                    if nxt and ch in PASS_2:
                        scores_2(g + 1, PASS_2[ch], ln0)
                    if ch >= LAG:
                        down_mm(c2, ch - LAG)
                down_end(c2)

            iterations(pe, prologue, iteration)


def _constants():
    import numpy as np

    ident = np.eye(P, dtype=np.float32)
    pos = np.arange(N)
    dist = np.minimum(pos[None, :P] - pos[:P, None], 0).astype(np.float32)
    inv = (np.float32(1.0) / np.float32(10000.0) ** (np.arange(0, HD, 2, dtype=np.float32) / np.float32(HD))).astype(np.float32)
    angle = (pos.astype(np.float32)[None, :] * inv[:, None]).astype(np.float64)
    d = np.arange(HD)
    cos = np.cos(angle)[d % (HD // 2)]
    sin = np.sin(angle)[d % (HD // 2)] * np.where(d < HD // 2, -1.0, 1.0)[:, None]
    rope = np.stack([cos, sin], 1)[:, None] * HD ** -0.25
    rope = np.broadcast_to(rope, (HD, H, 2, N)).reshape(P, 2, N).astype(np.float32)
    ids = np.broadcast_to(np.arange(E, dtype=np.float32), (P, TB, E))
    key, query = np.where(pos < P, pos - (P - 1), 0), np.where(pos >= P, (P - 1) - pos, 0)
    far = np.broadcast_to(np.stack([key, query]).astype(np.float32), (H, 2, N))
    rows = np.stack([pos >= P] * 3 + [pos < P] * 3 + [pos >= 0] * 2).astype(np.dtype("bfloat16"))
    rows = np.broadcast_to(rows[:, None, :], (8, H, N))
    return [np.ascontiguousarray(a) for a in (ident, dist, dist.T, rope, ids, far, rows)]


def kernel(L0_attn_x, L0_attn_qkv_w, L0_attn_proj_w, L0_attn_proj_b, L0_attn_slopes, L0_ffn_router_w, L0_ffn_w1,
           L0_ffn_v1, L0_ffn_w2, L0_ffn_bias):
    import concourse.bacc as bacc
    import numpy as np
    from concourse.bass_utils import run_bass_kernel_spmd

    qkv = np.asarray(L0_attn_qkv_w).reshape(3, H, HD, D)
    q, k = qkv[0].transpose(1, 0, 2), qkv[1].transpose(1, 0, 2)
    blocks = [q, k, np.roll(q, HD // 2, 0), np.roll(k, HD // 2, 0)]
    small = [b.reshape(P, D).T for b in blocks] + [qkv[2].reshape(P, D).T, np.asarray(L0_attn_proj_w).T,
                                                   np.asarray(L0_ffn_router_w)]
    ident, dist, dist_t, rope, ids, far, rows = _constants()
    arrays = {
        "x": L0_attn_x, "small_w": np.concatenate(small, 1), "w1": L0_ffn_w1, "v1": L0_ffn_v1, "w2": L0_ffn_w2,
        "ffn_bias": L0_ffn_bias, "proj_b": L0_attn_proj_b, "slopes": L0_attn_slopes, "ident": ident, "dist": dist,
        "dist_t": dist_t, "rope": rope, "expert_ids": ids, "far": far, "ones_rows": rows,
    }
    arrays = {"in_" + n: np.ascontiguousarray(a) for n, a in arrays.items()}
    nc = bacc.Bacc("TRN2", target_bir_lowering=False, num_devices=1)
    args = [nc.dram_tensor(n, a.shape, mybir.dt.from_np(a.dtype), kind="ExternalInput").ap() for n, a in arrays.items()]
    out = nc.dram_tensor("out", (B, N, D), F32, kind="ExternalOutput").ap()
    macaron(nc, *args, out)
    return run_bass_kernel_spmd(nc, [arrays], core_ids=[0]).results[0]["out"]
```

```python
from contextlib import ExitStack

import concourse.bass as bass
from concourse import mybir

F32 = mybir.dt.float32
F32R = mybir.dt.float32r
BF16 = mybir.dt.bfloat16
U32 = mybir.dt.uint32
ALU = mybir.AluOpType
ACT = mybir.ActivationFunctionType

B, N, D = 8, 256, 128
P = 128
TB = N // P
H, HD = 16, 8
E, F = 8, 352
UNITS = E * TB
FT = E * F
CH = FT // P
EPS = 1e-5
VW = 32
PAIRS = [(0, 0), (1, 0), (2, 0), (0, 1), (1, 1), (0, 2)]
QK_ROWS = len(PAIRS) * HD
S_ROWS = QK_ROWS + 6
E_ROWS = S_ROWS + 2
ROUTE = 10
LAG = 3
UP_FIRST = 2
DOWN_PIECES = 4
DOWN_STARTS = [k * CH // DOWN_PIECES for k in range(DOWN_PIECES + 1)]
PASS_1 = {ch: (ch - 5) // 2 for ch in range(5, CH, 2)}
PASS_1_UP = {u: len(PASS_1) + u for u in range(16 - len(PASS_1))}
P2_AT = 6
PASS_2 = {P2_AT + j * (CH - 1 - P2_AT) // 15: j for j in range(16)}
PASS_2_END = {ch: ch for ch in range(16)}
S1_AT = 14
AT = dict(
    T1=2, qk=4, rotate=3, part_0=6, part_1=8, pv_0=6, copy_0=5, oT_0=9, norm_0=8, pv_1=11, copy_1=11, oT_1=14,
    norm_1=12, v=15, values=15,
    aT=0, project=4, add=4, apply_2=6, T2=10, top_1=12, logits_1=14, rexp_1=14, gate_1=18,
    negate=8, max_T=10, stats_0=8, apply_0=10, T0=13, logits_0=15, top_0=14, rexp_0=15,
    gate_0=1, stats_1=13, apply_1=16,
)

CQ, CK, CV, CP, CR, CEND = 0, 128, 256, 384, 512, 520


def macaron(nc, x, small_w, w1, v1, w2, ffn_bias, proj_b, slopes, ident, dist, dist_t, rope, expert_ids,
            far, ones_rows, out):
    ctx = ExitStack()
    with ctx:
        ctx.enter_context(nc.allow_low_precision(reason="exact splits"))

        def sb(name, shape, dt=F32):
            return ctx.enter_context(nc.sbuf_tensor(name, shape, dt))

        def sem(name):
            return ctx.enter_context(nc.semaphore(name))

        xres = sb("xres", [P, B * TB, D])
        wup_hi, wup_lo = sb("wup_hi", [D, E, 2 * F], F32R), sb("wup_lo", [D, E, 2 * F], F32R)
        wdn_hi, wdn_lo = sb("wdn_hi", [P, CH, D], F32R), sb("wdn_lo", [P, CH, D], F32R)
        wsm_hi, wsm_lo = sb("wsm_hi", [D, CEND], F32R), sb("wsm_lo", [D, CEND], F32R)
        stage = sb("stage", [P, E * 2 * F + CH * D])
        stage_up = stage[:, 0:E * 2 * F].rearrange("p (e f) -> p e f", e=E)
        stage_dn = stage[:, E * 2 * F:].rearrange("p (c d) -> p c d", c=CH)
        probs = stage[:, 0:TB * H * N].rearrange("p (k h n) -> p k h n", k=TB, h=H)
        idn = sb("idn", [P, P])
        near = sb("near", [P, H + 2, P])
        near_t = sb("near_t", [P, H, P])
        dist_sb, dist_t_sb = sb("dist_sb", [P, P]), sb("dist_t_sb", [P, P])
        slope_bc = sb("slope_bc", [P, H])
        rope_sb = sb("rope_sb", [P, 2, N])
        ids = sb("ids", [P, TB, E])
        half_bias = sb("half_bias", [D, 1])
        fbias = sb("fbias", [D, 1])
        pb_row = sb("pb_row", [1, D])
        one_row = sb("one_row", [1, P])
        mhalf = sb("mhalf", [P, TB])
        slope_col = sb("slope_col", [H, 1])
        hid = sb("hid", [P, TB, FT])
        stage_sm = hid[:, 0, 0:CEND]
        gel = sb("gel", [P, 2, F])
        hT_hi, hT_lo = sb("hT_hi", [P, 4, N], F32R), sb("hT_lo", [P, 4, N], F32R)
        yT = sb("yT", [D, N])
        bst = [sb(f"bst{w}", [P, TB, 6]) for w in range(3)]
        mv = [sb(f"mv{w}", [P, TB, 2]) for w in range(3)]
        veps = [sb(f"veps{w}", [P, TB]) for w in range(3)]
        rstd = [sb(f"rstd{w}", [P, TB]) for w in range(3)]
        xn = sb("xn", [P, TB, D])
        xT_hi = [sb(f"xT_hi{w}", [D, N], F32R) for w in range(3)]
        xT_lo = [sb(f"xT_lo{w}", [D, N], F32R) for w in range(3)]
        top = [sb(f"top{w}", [P, TB, 8]) for w in range(2)]
        ix = [sb(f"ix{w}", [P, TB, 8], U32) for w in range(2)]
        ixf = [sb(f"ixf{w}", [P, TB, 2]) for w in range(2)]
        nmx = [sb(f"nmx{w}", [P, TB]) for w in range(2)]
        ex = [sb(f"ex{w}", [P, TB, 8]) for w in range(2)]
        sm = [sb(f"sm{w}", [P, TB]) for w in range(2)]
        rs = [sb(f"rs{w}", [P, TB]) for w in range(2)]
        wts = [sb(f"wts{w}", [P, TB, 2]) for w in range(2)]
        eq = [sb(f"eq{w}", [P, 2, TB, E]) for w in range(2)]
        gw = [sb(f"gw{w}", [P, 2, TB, E]) for w in range(2)]
        gate = [sb(f"gate{w}", [P, TB, E]) for w in range(2)]
        rc = sb("rc", [P, 2, N])
        lev = sb("lev", [P, 3, 2, N], BF16)
        qs, ks = sb("qs", [E_ROWS, H, N], BF16), sb("ks", [E_ROWS, H, N], BF16)
        vaug = sb("vaug", [P, TB, H, VW])
        mx = sb("mx", [P, TB, H])
        nm = sb("nm", [P, TB, H])
        ml = sb("ml", [H, 2, N], BF16)
        oT = sb("oT", [P, 2 * N])
        rsn = oT[:, :].rearrange("p (s n) -> p s n", s=2)
        far_v, far_l = rsn[0:H], lev[0:H]
        rden = sb("rden", [P, 2, 4 * TB * 2, 1])
        att = xn
        aT_hi, aT_lo = xT_hi[1], xT_lo[1]

        d_lev = nc.dram_tensor("d_lev", (2, 3, P, N), BF16, kind="Internal").ap()
        d_far = nc.dram_tensor("d_far", (3, 2, H, N), BF16, kind="Internal").ap()
        d_max = nc.dram_tensor("d_max", (2, H, N), BF16, kind="Internal").ap()

        def pb(name):
            return ctx.enter_context(nc.psum_tensor(name, [P, 512], F32))

        psA, psV, psY = pb("psA"), pb("psV"), pb("psY")
        psA2, psV2 = pb("psA2"), pb("psV2")
        up_a, up_v = [psA, psA2], [psV, psV2]
        psT = [psA, psV, psA2, psV2]
        psS = [pb("psS0"), pb("psS1")]
        psM = pb("psM")

        score_banks = [*psS, psM]

        xin_landed, xrest_landed, small_landed, idn_landed, const_landed = (sem(n) for n in (
            "xin_landed", "xrest_landed", "small_landed", "idn_landed", "const_landed"))
        up_landed = [sem(f"up_landed{e}") for e in range(E)]
        down_landed = [sem(f"down_landed{k}") for k in range(DOWN_PIECES)]
        wsm_hi_done, wsm_lo_done = sem("wsm_hi_done"), sem("wsm_lo_done")
        wup_hi_done, wup_lo_done = sem("wup_hi_done"), sem("wup_lo_done")
        wdn_hi_done, wdn_lo_done = sem("wdn_hi_done"), sem("wdn_lo_done")
        pool_const, near_done, vaug_zeroed, far_step = (sem(n) for n in ("pool_const", "near_done", "vaug_zeroed", "far_step"))
        far_out, rows_landed = sem("far_out"), sem("rows_landed")
        half_done = sem("half_done")
        a_full, v_full, gelu_done, hid_done = sem("a_full"), sem("v_full"), sem("gelu_done"), sem("hid_done")
        hT_full, hT_hi_done, hT_lo_done, down_done = sem("hT_full"), sem("hT_hi_done"), sem("hT_lo_done"), sem("down_done")
        yT_copied, y_full = sem("yT_copied"), sem("y_full")
        y_added, x2_done = sem("y_added"), sem("x2_done")
        LNS = ("f1", "at", "f2")
        stats_done = [sem(f"stats_done_{w}") for w in LNS]
        mean_done = [sem(f"mean_done_{w}") for w in LNS]
        eps_done = [sem(f"eps_done_{w}") for w in LNS]
        rstd_done = [sem(f"rstd_done_{w}") for w in LNS]
        xn_done = [sem(f"xn_done_{w}") for w in LNS]
        xT_full = [sem(f"xT_full_{w}") for w in LNS]
        xT_hi_done = [sem(f"xT_hi_done_{w}") for w in LNS]
        xT_lo_done = [sem(f"xT_lo_done_{w}") for w in LNS]
        logit_full = [sem(f"logit_full{w}") for w in range(2)]
        route = [sem(f"route{w}") for w in range(2)]
        nmx_done = [sem(f"nmx_done{w}") for w in range(2)]
        ex_done = [sem(f"ex_done{w}") for w in range(2)]
        gate_done = [sem(f"gate_done{w}") for w in range(2)]
        v_psum, v_copied = sem("v_psum"), sem("v_copied")
        qk_full, cos_done, sin_done = sem("qk_full"), sem("cos_done"), sem("sin_done")
        split_step, lev_out, stack_landed = sem("split_step"), sem("lev_out"), sem("stack_landed")
        s1_full, max_found = sem("s1_full"), sem("max_found")
        nm_done, mT_full, ml_hi, ml_done, ml_out, mrow_landed = (sem(n) for n in (
            "nm_done", "mT_full", "ml_hi", "ml_done", "ml_out", "mrow_landed"))
        s2_full, s2_biased, exp_done = sem("s2_full"), sem("s2_biased"), sem("exp_done")
        pv_full, oT_copied, o_full, rden_done, att_done = (sem(n) for n in (
            "pv_full", "oT_copied", "o_full", "rden_done", "att_done"))
        aT_full, aT_hi_done, aT_lo_done, proj_full = (sem(n) for n in ("aT_full", "aT_hi_done", "aT_lo_done", "proj_full"))
        stored = sem("stored")

        w1_v, v1_v = w1.rearrange("e d f -> d e f"), v1.rearrange("e d f -> d e f")
        w2_v = w2.rearrange("e f d -> (e f) d").rearrange("(c p) d -> p c d", p=P)
        out_v = out.rearrange("b (t p) d -> b p t d", p=P)
        block = ctx.enter_context(nc.Block())

        awaited = {}

        def const_first(eng, const_sem, const, by_batch_sem, value):
            if not isinstance(value, int):
                if eng not in awaited:
                    awaited[eng] = eng.alloc_register("awaited")
                eng.reg_mov(awaited[eng], value)
                value = awaited[eng]
            eng.wait_ge(const_sem, const)
            eng.wait_ge(by_batch_sem, value)

        def iterations(eng, prologue, iteration, ending):
            prologue()
            with eng.Fori(0, B - 3) as g:
                iteration(g, True)
            iteration(B - 3, False)
            ending()

        def call_1(g):
            return g * 2 + 2

        def call_2(g):
            return g * 2 + 3

        PENULT, LAST = B - 2, B - 1
        CALL_P, CALL_L = 2 * B - 2, 2 * B - 1

        def first(c):
            return isinstance(c, int) and c == 0

        @block.sync
        def _(sp):
            sp.dma_start(xres[:, 0:TB, :], x[0].rearrange("(t p) d -> p t d", p=P)).then_inc(xin_landed, 16)
            sp.dma_start(idn[:, :], ident).then_inc(idn_landed, 16)
            for e in range(E):
                sp.dma_start(stage_up[:, e, 0:F], w1_v[:, e, :]).then_inc(up_landed[e], 16)
                sp.dma_start(stage_up[:, e, F:2 * F], v1_v[:, e, :]).then_inc(up_landed[e], 16)
                if e == 0:
                    sp.dma_start(ids[:, :, :], expert_ids).then_inc(idn_landed, 16)
                if e == 2:
                    sp.dma_start(fbias[:, :], ffn_bias.rearrange("(d o) -> d o", o=1)).then_inc(pool_const, 16)
                    sp.dma_start(slope_bc[:, :], slopes.partition_broadcast(P)).then_inc(pool_const, 16)
                    sp.dma_start(dist_sb[:, :], dist).then_inc(pool_const, 16)
                    sp.dma_start(dist_t_sb[:, :], dist_t).then_inc(pool_const, 16)
            for k in range(DOWN_PIECES):
                c = slice(DOWN_STARTS[k], DOWN_STARTS[k + 1])
                sp.dma_start(stage_dn[:, c, :], w2_v[:, c, :]).then_inc(down_landed[k], 16)
            sp.dma_start(xres[:, TB:, :], x[1:].rearrange("b (t p) d -> p (b t) d", p=P)).then_inc(xrest_landed, 16)
            sp.dma_start(slope_col[:, :], slopes.rearrange("(h o) -> h o", o=1)).then_inc(pool_const, 16)
            sp.dma_start(far_v, far).then_inc(pool_const, 16)
            sp.dma_start(rope_sb[:, :, :], rope).then_inc(const_landed, 16)
            sp.dma_start(pb_row[:, :], proj_b.rearrange("(o d) -> o d", o=1)).then_inc(const_landed, 16)
            sp.dma_start(qs[QK_ROWS:QK_ROWS + 3, :, :], ones_rows[0:3]).then_inc(rows_landed, 16)
            sp.dma_start(ks[QK_ROWS + 3:E_ROWS, :, :], ones_rows[3:8]).then_inc(rows_landed, 16)
            sp.wait_ge(far_step, 5)
            sp.dma_start(d_far.rearrange("l s h n -> h l s n"), far_l).then_inc(far_out, 16)
            sp.wait_ge(far_out, 16)
            sp.dma_start(ks[QK_ROWS:QK_ROWS + 3, :, :], d_far[:, 0]).then_inc(rows_landed, 16)
            sp.dma_start(qs[QK_ROWS + 3:S_ROWS, :, :], d_far[:, 1]).then_inc(rows_landed, 16)

            def stack(b):
                sp.wait_ge(split_step, b * 5 + 5)
                for s in range(2):
                    sp.dma_start(d_lev[s].rearrange("l p n -> p l n"), lev[:, :, s, :]).then_inc(lev_out, 16)
                sp.wait_ge(lev_out, b * 32 + 32)
                if isinstance(b, int) and b == LAST:
                    sp.wait_ge(exp_done, b * 16)
                for s, dst in ((0, qs), (1, ks)):
                    for t, pair in enumerate(PAIRS):
                        sp.dma_start(dst[t * HD:(t + 1) * HD, :, :],
                                     d_lev[s, pair[s]].rearrange("(d h) n -> d h n", h=H)).then_inc(stack_landed, 16)

            def max_rows(b):
                sp.wait_ge(ml_done, b + 1)
                sp.dma_start(d_max.rearrange("l h n -> h l n"), ml[:, :, :]).then_inc(ml_out, 16)
                sp.wait_ge(ml_out, b * 16 + 16)
                sp.dma_start(qs[S_ROWS:E_ROWS, :, :], d_max).then_inc(mrow_landed, 16)

            def store(b, c):
                sp.wait_ge(y_added, c + 1)
                sp.dma_start(out_v[b], xres[:, bass.ds(b * TB, TB), :]).then_inc(stored, 16)

            def prologue():
                stack(0)
                max_rows(0)

            def iteration(g, ln0):
                stack(g + 1)
                max_rows(g + 1)
                if not ln0:
                    stack(g + 2)
                store(g, call_2(g))

            def ending():
                max_rows(LAST)
                store(PENULT, CALL_P)
                store(LAST, CALL_L)

            iterations(sp, prologue, iteration, ending)
            sp.wait_ge(stored, B * 16)

        @block.gpsimd
        def _(pool):
            nc.gpsimd.memset(mhalf[:, :], -0.5).then_inc(half_done, 1)

            def rstd_of(w, b):
                const_first(pool, half_done, 1, mean_done[w], b * TB + TB)
                nc.gpsimd.tensor_scalar(veps[w][:, :], mv[w][:, :, 1], EPS, None, ALU.add).then_inc(eps_done[w], 1)
                pool.wait_ge(eps_done[w], b + 1)
                nc.gpsimd.tensor_tensor(rstd[w][:, :], veps[w][:, :], mhalf[:, :], ALU.pow).then_inc(rstd_done[w], 1)

            def split_qk(b):
                pool.wait_ge(cos_done, b + 1)
                pool.wait_ge(sin_done, b * 2 + 2)
                nc.gpsimd.tensor_tensor(rc[:, :, :], rc[:, :, :], rsn, ALU.add).then_inc(split_step, 1)
                pool.wait_ge(split_step, b * 5 + 2)
                nc.gpsimd.tensor_tensor(rc[:, :, :], rc[:, :, :], lev[:, 0], ALU.subtract).then_inc(split_step, 1)
                pool.wait_ge(split_step, b * 5 + 4)
                nc.gpsimd.tensor_tensor(lev[:, 2], rc[:, :, :], lev[:, 1], ALU.subtract).then_inc(split_step, 1)

            def prologue():
                rstd_of(0, 0)
                nc.gpsimd.memset(one_row[:, :], 1.0)
                nc.gpsimd.memset(near[:, :, :], 0.0)
                nc.gpsimd.memset(vaug[:, :, :, :], 0.0).then_inc(vaug_zeroed, 1)
                pool.wait_ge(vaug_zeroed, 1)
                nc.gpsimd.memset(vaug[:, :, :, HD:HD + 1], 1.0)
                for k in range(DOWN_PIECES):
                    c = slice(DOWN_STARTS[k], DOWN_STARTS[k + 1])
                    pool.wait_ge(wdn_hi_done, k + 1)
                    nc.gpsimd.tensor_tensor(wdn_lo[:, c, :], stage_dn[:, c, :], wdn_hi[:, c, :].bitcast(F32), ALU.subtract
                                            ).then_inc(wdn_lo_done, 1)
                pool.wait_ge(pool_const, 96)
                nc.gpsimd.tensor_scalar(half_bias[:, :], fbias[:, :], 0.5, None, ALU.mult).then_inc(half_done, 1)
                rstd_of(0, 1)
                nc.gpsimd.tensor_scalar(far_v, far_v, slope_col[:, :], 8.0, ALU.mult, ALU.mult).then_inc(far_step, 1)
                pool.wait_ge(far_step, 1)
                nc.gpsimd.tensor_copy(far_l[:, 0], far_v).then_inc(far_step, 1)
                pool.wait_ge(far_step, 2)
                nc.gpsimd.tensor_tensor(far_v, far_v, far_l[:, 0], ALU.subtract).then_inc(far_step, 1)
                pool.wait_ge(far_step, 3)
                nc.gpsimd.tensor_copy(far_l[:, 1], far_v).then_inc(far_step, 1)
                pool.wait_ge(far_step, 4)
                nc.gpsimd.tensor_tensor(far_l[:, 2], far_v, far_l[:, 1], ALU.subtract).then_inc(far_step, 1)
                for h in range(H):
                    if h == 10:
                        rstd_of(1, 0)
                    nc.gpsimd.tensor_scalar(near[:, h + 1, :], dist_sb[:, :], slope_bc[:, h:h + 1], 8.0,
                                            ALU.mult, ALU.mult).then_inc(near_done, 1)
                    nc.gpsimd.tensor_scalar(near_t[:, h, :], dist_t_sb[:, :], slope_bc[:, h:h + 1], 8.0,
                                            ALU.mult, ALU.mult).then_inc(near_done, 1)
                pool.wait_ge(far_out, 16)
                rstd_of(0, 2)
                split_qk(0)
                rstd_of(1, 1)

            def iteration(g, ln0):
                split_qk(g + 1)
                rstd_of(2, g)
                if ln0:
                    rstd_of(0, g + 3)
                    rstd_of(1, g + 2)
                else:
                    rstd_of(1, g + 2)
                    split_qk(g + 2)

            def ending():
                rstd_of(2, PENULT)
                rstd_of(2, LAST)

            iterations(pool, prologue, iteration, ending)

        @block.scalar
        def _(act):
            act.dma_start(stage_sm, small_w).then_inc(small_landed, 16)
            copy, gelu, exp, ident_f = ACT.Copy, ACT.Gelu, ACT.Exp, ACT.Identity

            def xT_high(w, b):
                act.wait_ge(xT_full[w], b + 1)
                nc.scalar.activation(xT_hi[w][:, :], psM[:, 0:N], copy).then_inc(xT_hi_done[w], 1)

            def router_exp(r, b):
                act.wait_ge(nmx_done[r], b + 1)
                for t in range(TB):
                    nc.scalar.activation(ex[r][:, t, :], top[r][:, t, :], exp, bias=nmx[r][:, t:t + 1],
                                         accum_out=sm[r][:, t:t + 1]).then_inc(ex_done[r], 1)

            def gate_gelu(c, u):
                act.wait_ge(a_full, c * UNITS + (u + 1))
                if u >= 2 or not first(c):
                    act.wait_ge(hid_done, c * UNITS + (u - 1))
                nc.scalar.activation(gel[:, u % 2, :], up_a[u % 2][:, 0:F], gelu).then_inc(gelu_done, 1)

            def hid_high(c, ch):
                act.wait_ge(hT_full, c * CH + (ch + 1))
                if ch == 0 and not first(c):
                    act.wait_ge(down_done, c * CH)
                if ch >= 4:
                    act.wait_ge(down_done, c * CH + (ch - 3))
                nc.scalar.activation(hT_hi[:, ch % 4, :], psT[ch % 4][:, 0:N], copy).then_inc(hT_hi_done, 1)

            def y_copy(c):
                act.wait_ge(down_done, c * CH + CH)
                nc.scalar.activation(yT[:, :], psY[:, 0:N], ident_f, bias=half_bias[:, 0:1]).then_inc(yT_copied, 1)

            def values(b):
                act.wait_ge(v_psum, b + 1)
                nc.scalar.activation(vaug[:, :, :, 0:HD],
                                     psM[:, N:2 * N].rearrange("p (t h d) -> p t h d", t=TB, h=H), copy).then_inc(v_copied, 1)

            def part(b, level):
                act.wait_ge(split_step, b * 5 + (2 * level + 1))
                nc.scalar.activation(lev[:, level], rc[:, :, :], copy).then_inc(split_step, 1)

            def max_high(b):
                act.wait_ge(mT_full, b + 1)
                nc.scalar.activation(ml[:, 0, :], psM[0:H, 0:N], copy).then_inc(ml_hi, 1)

            def attention_exp(b, j):
                act.wait_ge(s2_biased, b * 16 + (j + 1))
                hp, kt = j // 2, j % 2
                nc.scalar.activation(probs[:, kt, 2 * hp:2 * hp + 2, :],
                                     score_banks[j % 3][:, :].rearrange("p (h n) -> p h n", h=2), exp).then_inc(exp_done, 1)

            def oT_copy(b, half, split=0):
                act.wait_ge(pv_full, b * 2 + (half + 1))
                if half == 0 and split:
                    act.wait_ge(split_step, b * 5 + 6)
                nc.scalar.activation(oT[:, :], psM[:, :], copy).then_inc(oT_copied, 1)

            def aT_high(b):
                act.wait_ge(aT_full, b + 1)
                nc.scalar.activation(aT_hi[:, :], psM[:, 0:N], copy).then_inc(aT_hi_done, 1)

            def prologue():
                act.wait_ge(small_landed, 16)
                nc.scalar.activation(wsm_hi[:, :], stage_sm, copy).then_inc(wsm_hi_done, 1)
                xT_high(0, 0)

                def up_high(e):
                    act.wait_ge(up_landed[e], 32)
                    nc.scalar.activation(wup_hi[:, e, :], stage_up[:, e, :], copy).then_inc(wup_hi_done, 1)

                up_high(0)
                router_exp(0, 0)
                for e in range(E):
                    if e + 1 < E:
                        up_high(e + 1)
                    for u in (2 * e, 2 * e + 1):
                        gate_gelu(0, u)
                    k = e - 3
                    if 0 <= k < DOWN_PIECES:
                        c = slice(DOWN_STARTS[k], DOWN_STARTS[k + 1])
                        act.wait_ge(down_landed[k], 16)
                        nc.scalar.activation(wdn_hi[:, c, :], stage_dn[:, c, :], copy).then_inc(wdn_hi_done, 1)
                for ch in range(CH):
                    hid_high(0, ch)
                    if ch == 8:
                        xT_high(0, 1)
                    if ch == 12:
                        router_exp(0, 1)
                act.wait_ge(half_done, 2)
                y_copy(0)
                for u in range(UNITS):
                    gate_gelu(1, u)
                    if u == 4:
                        xT_high(1, 0)
                    if u == 6:
                        values(0)
                    if u == 11:
                        act.wait_ge(far_out, 16)
                        part(0, 0)
                    if u == 13:
                        part(0, 1)
                for ch in range(CH):
                    hid_high(1, ch)
                    if ch == 3:
                        xT_high(0, 2)
                    if ch == 8:
                        router_exp(0, 2)
                y_copy(1)
                max_high(0)
                for j in range(16):
                    attention_exp(0, j)
                gate_gelu(2, 0)

            def iteration(g, ln0):
                c1, c2 = call_1(g), call_2(g)
                for u in range(UNITS):
                    if u:
                        gate_gelu(c1, u)
                    if u == AT["T1"]:
                        xT_high(1, g + 1)
                    if u == AT["copy_0"]:
                        oT_copy(g, 0, split=True)
                    if u == AT["part_0"]:
                        part(g + 1, 0)
                    if u == AT["part_1"]:
                        part(g + 1, 1)
                    if u == AT["copy_1"]:
                        oT_copy(g, 1)
                    if u == AT["values"]:
                        values(g + 1)
                for ch in range(CH):
                    hid_high(c1, ch)
                    if ch == AT["aT"]:
                        aT_high(g)
                    if ch == AT["T2"]:
                        xT_high(2, g)
                    if ch == AT["rexp_1"]:
                        router_exp(1, g)
                gate_gelu(c2, 0)
                y_copy(c1)
                for u in range(UNITS):
                    if u:
                        gate_gelu(c2, u)
                    if u == AT["max_T"]:
                        max_high(g + 1)
                    if ln0 and u == AT["T0"]:
                        xT_high(0, g + 3)
                    if not ln0 and u == AT["T0"]:
                        xT_high(1, g + 2)
                    if ln0 and u == AT["rexp_0"]:
                        router_exp(0, g + 3)
                for ch in range(CH):
                    hid_high(c2, ch)
                    if not ln0 and ch in (3, 6):
                        part(g + 2, ch // 3 - 1)
                    if ch - 1 in PASS_2:
                        attention_exp(g + 1, PASS_2[ch - 1])
                attention_exp(g + 1, 15)
                if ln0:
                    gate_gelu(call_1(g + 1), 0)
                y_copy(c2)

            def ending():
                oT_copy(PENULT, 0, split=True)
                oT_copy(PENULT, 1)
                values(LAST)
                aT_high(PENULT)
                xT_high(2, PENULT)
                router_exp(1, PENULT)
                for u in range(UNITS):
                    gate_gelu(CALL_P, u)
                    if u == 3:
                        max_high(LAST)
                for ch in range(CH):
                    hid_high(CALL_P, ch)
                    if ch - 1 in PASS_2_END:
                        attention_exp(LAST, PASS_2_END[ch - 1])
                    if ch == 18:
                        oT_copy(LAST, 0)
                y_copy(CALL_P)
                oT_copy(LAST, 1)
                aT_high(LAST)
                xT_high(2, LAST)
                router_exp(1, LAST)
                for u in range(UNITS):
                    gate_gelu(CALL_L, u)
                for ch in range(CH):
                    hid_high(CALL_L, ch)
                y_copy(CALL_L)

            iterations(act, prologue, iteration, ending)

        @block.vector
        def _(dve):
            def ln_stats(w, b):
                for t in range(TB):
                    nc.vector.bn_stats(bst[w][:, t, :], xres[:, b * TB + t, :]).then_inc(stats_done[w], 1)
                for t in range(TB):
                    const_first(dve, xin_landed, 16, stats_done[w], b * TB + (t + 1))
                    nc.vector.bn_aggr(mv[w][:, t, :], bst[w][:, t, :]).then_inc(mean_done[w], 1)

            def ln_apply(w, b):
                dve.wait_ge(rstd_done[w], b + 1)
                for t in range(TB):
                    nc.vector.tensor_scalar(xn[:, t, :], xres[:, b * TB + t, :], mv[w][:, t, 0:1], rstd[w][:, t:t + 1],
                                            ALU.subtract, ALU.mult).then_inc(xn_done[w], 1)

            def xT_low(w, b):
                dve.wait_ge(xT_hi_done[w], b + 1)
                nc.vector.tensor_tensor(xT_lo[w][:, :], psM[:, 0:N], xT_hi[w][:, :].bitcast(F32), ALU.subtract).then_inc(
                    xT_lo_done[w], 1)

            def route_top(r, b):
                const_first(dve, idn_landed, 32, logit_full[r], b + 1)
                for t in range(TB):
                    nc.vector.max(top[r][:, t, :], psM[:, N + 8 * t:N + 8 * t + 8]).then_inc(route[r], 1)
                dve.wait_ge(route[r], b * ROUTE + 2)
                nc.vector.tensor_scalar(nmx[r][:, :], top[r][:, :, 0], -1.0, None, ALU.mult).then_inc(nmx_done[r], 1)
                for t in range(TB):
                    nc.vector.max_index(ix[r][:, t, :], top[r][:, t, :], psM[:, N + 8 * t:N + 8 * t + 8]).then_inc(route[r], 1)
                dve.wait_ge(route[r], b * ROUTE + 4)
                nc.vector.tensor_copy(ixf[r][:, :, :], ix[r][:, :, 0:2]).then_inc(route[r], 1)

            def route_gate(r, b):
                dve.wait_ge(route[r], b * ROUTE + 5)
                nc.vector.tensor_tensor(eq[r][:, :, :, :], ids[:, None, :, :].broadcast_to([P, 2, TB, E]),
                                        ixf[r][:, :, :].rearrange("p t k -> p k t")[:, :, :, None].broadcast_to([P, 2, TB, E]),
                                        ALU.is_equal).then_inc(route[r], 1)
                dve.wait_ge(ex_done[r], b * TB + TB)
                nc.vector.tensor_scalar(sm[r][:, :], sm[r][:, :], 2.0, None, ALU.mult).then_inc(route[r], 1)
                dve.wait_ge(route[r], b * ROUTE + 7)
                nc.vector.reciprocal(rs[r][:, :], sm[r][:, :]).then_inc(route[r], 1)
                dve.wait_ge(route[r], b * ROUTE + 8)
                nc.vector.tensor_tensor(wts[r][:, :, :], ex[r][:, :, 0:2], rs[r][:, :, None].broadcast_to([P, TB, 2]),
                                        ALU.mult).then_inc(route[r], 1)
                dve.wait_ge(route[r], b * ROUTE + 9)
                nc.vector.tensor_tensor(gw[r][:, :, :, :], eq[r][:, :, :, :],
                                        wts[r][:, :, :].rearrange("p t k -> p k t")[:, :, :, None].broadcast_to([P, 2, TB, E]),
                                        ALU.mult).then_inc(route[r], 1)
                dve.wait_ge(route[r], b * ROUTE + 10)
                nc.vector.tensor_tensor(gate[r][:, :, :], gw[r][:, 0], gw[r][:, 1], ALU.add).then_inc(gate_done[r], 1)

            def gated(r, b, c, u):
                e, t = u // TB, u % TB
                if u == 0:
                    dve.wait_ge(gate_done[r], b + 1)
                    if not first(c):
                        dve.wait_ge(hT_full, c * CH)
                dve.wait_ge(gelu_done, c * UNITS + (u + 1))
                dve.wait_ge(v_full, c * UNITS + (u + 1))
                nc.vector.scalar_tensor_tensor(out=hid[:, t, e * F:(e + 1) * F], in0=up_v[u % 2][:, 0:F],
                                               scalar=gate[r][:, t, e:e + 1], in1=gel[:, u % 2, :],
                                               op0=ALU.mult, op1=ALU.mult).then_inc(hid_done, 1)

            def hid_low(c, ch):
                dve.wait_ge(hT_hi_done, c * CH + (ch + 1))
                nc.vector.tensor_tensor(hT_lo[:, ch % 4, :], psT[ch % 4][:, 0:N], hT_hi[:, ch % 4, :].bitcast(F32), ALU.subtract
                                        ).then_inc(hT_lo_done, 1)

            def y_add(c, b):
                dve.wait_ge(y_full, c + 1)
                nc.vector.tensor_tensor(xres[:, bass.ds(b * TB, TB), :], xres[:, bass.ds(b * TB, TB), :],
                                        psY[:, N:2 * N].rearrange("p (t d) -> p t d", t=TB), ALU.add).then_inc(y_added, 1)

            def rotate(b):
                dve.wait_ge(qk_full, b + 1)
                if not (isinstance(b, int) and b == 0):
                    dve.wait_ge(split_step, b * 5)
                nc.vector.tensor_tensor(rc[:, :, :], psM[:, :].rearrange("p (s n) -> p s n", s=2), rope_sb[:, 0:1, :].broadcast_to([P, 2, N]), ALU.mult
                                        ).then_inc(cos_done, 1)

            def rotate_2(b):
                for half in range(2):
                    src, dst = slice(half * 64, half * 64 + 64), slice(64 - half * 64, 128 - half * 64)
                    nc.vector.tensor_tensor(rsn[dst], psM[src, :].rearrange("p (s n) -> p s n", s=2),
                                            rope_sb[src, 1:2, :].broadcast_to([64, 2, N]), ALU.mult).then_inc(sin_done, 1)

            def row_max(b, i):
                qt, hp = i // 8, i % 8
                const_first(dve, near_done, 2 * H, s1_full, b * 16 + (i + 1))
                for j in range(2):
                    h = 2 * hp + j
                    bias = near[:, h + 1:H + 2:H - h, :] if qt == 0 else near[:, 0:h + 2:h + 1, :]
                    part = psS[i % 2][:, j * N:(j + 1) * N].rearrange("p (a n) -> p a n", a=TB)
                    nc.vector.tensor_tensor_reduce(out=part, in0=part, in1=bias,
                                                   scale=1.0, scalar=-3.0e38, op0=ALU.add, op1=ALU.max,
                                                   accum_out=mx[:, qt, h:h + 1]).then_inc(max_found, 1)

            def max_negate(b):
                dve.wait_ge(max_found, b * 32 + 32)
                nc.vector.tensor_scalar(nm[:, :, :], mx[:, :, :], -1.0, None, ALU.mult).then_inc(nm_done, 1)

            def max_low(b):
                dve.wait_ge(ml_hi, b + 1)
                nc.vector.tensor_tensor(ml[:, 1, :], psM[0:H, 0:N], ml[:, 0, :], ALU.subtract).then_inc(ml_done, 1)

            def near_bias(b, j):
                hp, kt = j // 2, j % 2
                dve.wait_ge(s2_full, b * 16 + (j + 1))
                part = score_banks[j % 3][:, :].rearrange("p (h n) -> p h n", h=2)[:, :, kt * P:(kt + 1) * P]
                nc.vector.tensor_tensor(part, part, near_t[:, 2 * hp:2 * hp + 2, :], ALU.add).then_inc(s2_biased, 1)

            def normalize(b, half):
                dve.wait_ge(o_full, b * 2 + (half + 1))
                nc.vector.reciprocal(rden[:, half], psM[:, :].rearrange("p (x v) -> p x v", v=VW)[:, :, HD:HD + 1]
                                     ).then_inc(rden_done, 1)
                dve.wait_ge(rden_done, b * 2 + (half + 1))
                for qt in range(TB):
                    o = psM[:, :].rearrange("p (a q j v) -> p a q j v", a=2, q=TB, j=4)[:, :, qt, :, 0:HD]
                    r = rden[:, half].rearrange("p (a q j) o -> p a q j o", a=2, q=TB)[:, :, qt, :, :].broadcast_to([P, 2, 4, HD])
                    nc.vector.tensor_tensor(att[:, qt, half * 64:(half + 1) * 64].rearrange("p (a j d) -> p a j d", a=2, j=4),
                                            o, r, ALU.mult).then_inc(att_done, 1)

            def aT_low(b):
                dve.wait_ge(aT_hi_done, b + 1)
                nc.vector.tensor_tensor(aT_lo[:, :], psM[:, 0:N], aT_hi[:, :].bitcast(F32), ALU.subtract).then_inc(aT_lo_done, 1)

            def attention_add(b):
                dve.wait_ge(proj_full, b + 1)
                nc.vector.tensor_tensor(xres[:, bass.ds(b * TB, TB), :], xres[:, bass.ds(b * TB, TB), :],
                                        psM[:, 0:N].rearrange("p (t d) -> p t d", t=TB), ALU.add).then_inc(x2_done, 1)

            def prologue():
                dve.wait_ge(xin_landed, 16)
                ln_stats(0, 0)
                ln_apply(0, 0)
                dve.wait_ge(wsm_hi_done, 1)
                nc.vector.tensor_tensor(wsm_lo[:, :], stage_sm, wsm_hi[:, :].bitcast(F32), ALU.subtract).then_inc(wsm_lo_done, 1)
                xT_low(0, 0)

                def up_low(e):
                    dve.wait_ge(wup_hi_done, e + 1)
                    nc.vector.tensor_tensor(wup_lo[:, e, :], stage_up[:, e, :], wup_hi[:, e, :].bitcast(F32), ALU.subtract
                                            ).then_inc(wup_lo_done, 1)

                up_low(0)
                route_top(0, 0)
                route_gate(0, 0)
                for e in range(E):
                    if e + 1 < E:
                        up_low(e + 1)
                    for u in (2 * e, 2 * e + 1):
                        gated(0, 0, 0, u)
                dve.wait_ge(xrest_landed, 16)
                ln_stats(0, 1)
                for ch in range(CH):
                    hid_low(0, ch)
                    if ch == 6:
                        ln_apply(0, 1)
                    if ch == 8:
                        xT_low(0, 1)
                    if ch == 11:
                        route_top(0, 1)
                    if ch == 15:
                        route_gate(0, 1)
                y_add(0, 0)
                for u in range(UNITS):
                    gated(0, 1, 1, u)
                    if u == 0:
                        dve.wait_ge(y_added, 1)
                        ln_stats(1, 0)
                    if u == 2:
                        ln_apply(1, 0)
                    if u == 4:
                        xT_low(1, 0)
                    if u == 5:
                        ln_stats(0, 2)
                    if u == 7:
                        dve.wait_ge(const_landed, 32)
                        rotate(0)
                    if u == 8:
                        dve.wait_ge(far_step, 5)
                        rotate_2(0)
                    if u == 15:
                        ln_apply(0, 2)
                for ch in range(CH):
                    hid_low(1, ch)
                    if ch == 3:
                        xT_low(0, 2)
                    if ch == 6:
                        route_top(0, 2)
                    if ch == 10:
                        route_gate(0, 2)
                    if ch >= S1_AT:
                        row_max(0, ch - S1_AT)
                y_add(1, 1)
                for i in range(CH - S1_AT, 16):
                    row_max(0, i)
                max_negate(0)
                max_low(0)
                dve.wait_ge(y_added, 2)
                ln_stats(1, 1)
                for j in range(16):
                    near_bias(0, j)
                ln_apply(1, 1)
                gated(0, 2, 2, 0)

            def iteration(g, ln0):
                c1, c2 = call_1(g), call_2(g)
                for u in range(UNITS):
                    if u:
                        gated(0, g + 2, c1, u)
                    if u == AT["T1"]:
                        xT_low(1, g + 1)
                    if u == AT["rotate"]:
                        rotate(g + 1)
                        rotate_2(g + 1)
                    if u == AT["norm_0"]:
                        normalize(g, 0)
                    if u == AT["norm_1"]:
                        normalize(g, 1)
                for ch in range(CH):
                    hid_low(c1, ch)
                    if ch == AT["aT"]:
                        aT_low(g)
                    if ch == AT["add"]:
                        attention_add(g)
                        const_first(dve, xin_landed, 16, x2_done, g + 1)
                        ln_stats(2, g)
                    if ch == AT["apply_2"]:
                        ln_apply(2, g)
                    if ch == AT["T2"]:
                        xT_low(2, g)
                    if ch == AT["top_1"]:
                        route_top(1, g)
                    if ch == AT["gate_1"]:
                        route_gate(1, g)
                    if ch in PASS_1:
                        row_max(g + 1, PASS_1[ch])
                gated(1, g, c2, 0)
                y_add(c1, g + 2)
                for u in range(UNITS):
                    if u:
                        gated(1, g, c2, u)
                    if u in PASS_1_UP:
                        row_max(g + 1, PASS_1_UP[u])
                    if u == AT["negate"]:
                        max_negate(g + 1)
                    if ln0 and u == AT["stats_0"]:
                        ln_stats(0, g + 3)
                    if not ln0 and u == AT["stats_0"]:
                        const_first(dve, xin_landed, 16, y_added, c1 + 1)
                        ln_stats(1, g + 2)
                    if u == AT["max_T"]:
                        max_low(g + 1)
                    if ln0 and u == AT["apply_0"]:
                        ln_apply(0, g + 3)
                    if not ln0 and u == AT["apply_0"]:
                        ln_apply(1, g + 2)
                    if ln0 and u == AT["T0"]:
                        xT_low(0, g + 3)
                    if not ln0 and u == AT["T0"]:
                        xT_low(1, g + 2)
                    if not ln0 and u == AT["T0"] + 2:
                        rotate(g + 2)
                        rotate_2(g + 2)
                    if ln0 and u == AT["top_0"]:
                        route_top(0, g + 3)
                for ch in range(CH):
                    hid_low(c2, ch)
                    if ln0 and ch == AT["gate_0"]:
                        route_gate(0, g + 3)
                    if ln0 and ch == AT["stats_1"]:
                        const_first(dve, xin_landed, 16, y_added, c1 + 1)
                        ln_stats(1, g + 2)
                    if ln0 and ch == AT["apply_1"]:
                        ln_apply(1, g + 2)
                    if ch in PASS_2:
                        near_bias(g + 1, PASS_2[ch])
                if ln0:
                    gated(0, g + 3, call_1(g + 1), 0)
                y_add(c2, g)

            def ending():
                normalize(PENULT, 0)
                for i in range(16):
                    row_max(LAST, i)
                    if i == 1:
                        normalize(PENULT, 1)
                    if i == 5:
                        aT_low(PENULT)
                    if i == 7:
                        attention_add(PENULT)
                        dve.wait_ge(x2_done, PENULT + 1)
                        ln_stats(2, PENULT)
                    if i == 9:
                        ln_apply(2, PENULT)
                    if i == 11:
                        xT_low(2, PENULT)
                    if i == 13:
                        route_top(1, PENULT)
                max_negate(LAST)
                route_gate(1, PENULT)
                for u in range(UNITS):
                    gated(1, PENULT, CALL_P, u)
                    if u == 3:
                        max_low(LAST)
                for ch in range(CH):
                    hid_low(CALL_P, ch)
                    if ch in PASS_2_END:
                        near_bias(LAST, PASS_2_END[ch])
                    if ch == 20:
                        normalize(LAST, 0)
                y_add(CALL_P, PENULT)
                normalize(LAST, 1)
                aT_low(LAST)
                attention_add(LAST)
                dve.wait_ge(x2_done, LAST + 1)
                ln_stats(2, LAST)
                ln_apply(2, LAST)
                xT_low(2, LAST)
                route_top(1, LAST)
                route_gate(1, LAST)
                for u in range(UNITS):
                    gated(1, LAST, CALL_L, u)
                for ch in range(CH):
                    hid_low(CALL_L, ch)
                y_add(CALL_L, LAST)

            iterations(dve, prologue, iteration, ending)

        @block.tensor
        def _(pe):
            def mm3(o, l_hi, l_lo, r_hi, r_lo, start=True, stop=True):
                nc.tensor.matmul(o, l_hi, r_hi, start=start, stop=False)
                nc.tensor.matmul(o, l_hi, r_lo, start=False, stop=False)
                return nc.tensor.matmul(o, l_lo, r_hi, start=False, stop=stop)

            def ln_T(w, b):
                pe.wait_ge(xn_done[w], b * TB + TB)
                for t in range(TB):
                    i = nc.tensor.transpose(psM[:, t * P:(t + 1) * P], xn[:, t, :], idn[:, :])
                i.then_inc(xT_full[w], 1)

            def logits(r, b):
                w = 2 * r
                pe.wait_ge(xT_lo_done[w], b + 1)
                for t in range(TB):
                    s = slice(t * P, (t + 1) * P)
                    i = mm3(psM[:, N + 8 * t:N + 8 * t + 8], xT_hi[w][:, s], xT_lo[w][:, s], wsm_hi[:, CR:CEND], wsm_lo[:, CR:CEND])
                i.then_inc(logit_full[r], 1)

            def up_gate(r, c, u):
                e, t, w = u // TB, u % TB, 2 * r
                if u >= 2 or (u == 0 and not first(c)):
                    pe.wait_ge(gelu_done, c * UNITS + (u - 1))
                s = slice(t * P, (t + 1) * P)
                mm3(up_a[u % 2][:, 0:F], xT_hi[w][:, s], xT_lo[w][:, s], wup_hi[:, e, 0:F], wup_lo[:, e, 0:F]).then_inc(a_full, 1)

            def up_value(r, c, u):
                e, t, w = u // TB, u % TB, 2 * r
                if u >= 2 or (u == 0 and not first(c)):
                    pe.wait_ge(hid_done, c * UNITS + (u - 1))
                s = slice(t * P, (t + 1) * P)
                mm3(up_v[u % 2][:, 0:F], xT_hi[w][:, s], xT_lo[w][:, s], wup_hi[:, e, F:2 * F], wup_lo[:, e, F:2 * F]).then_inc(v_full, 1)

            def down_T(c, ch):
                if ch in (0, 2):
                    pe.wait_ge(hid_done, c * UNITS + (UNITS - 1 + ch // 2))
                if ch >= 4:
                    pe.wait_ge(hT_lo_done, c * CH + (ch - 3))
                for t in range(TB):
                    i = nc.tensor.transpose(psT[ch % 4][:, t * P:(t + 1) * P], hid[:, t, ch * P:(ch + 1) * P], idn[:, :])
                i.then_inc(hT_full, 1)

            def down_mm(c, ch):
                pe.wait_ge(hT_lo_done, c * CH + (ch + 1))
                if ch == 0 and not first(c):
                    pe.wait_ge(y_added, c)
                r_hi, r_lo = hT_hi[:, ch % 4, :], hT_lo[:, ch % 4, :]
                nc.tensor.matmul(psY[:, 0:N], wdn_hi[:, ch, :], r_hi, start=(ch == 0), stop=False)
                nc.tensor.matmul(psY[:, 0:N], wdn_hi[:, ch, :], r_lo, start=False, stop=False)
                nc.tensor.matmul(psY[:, 0:N], wdn_lo[:, ch, :], r_hi, start=False, stop=(ch == CH - 1)).then_inc(down_done, 1)

            def down_end(c, r=0, following=None):
                for ch in range(CH - LAG, CH):
                    if following is not None and ch == CH - 1:
                        up_gate(r, following, 0)
                    down_mm(c, ch)
                if following is not None:
                    up_value(r, following, 0)
                    for u in range(1, UP_FIRST):
                        up_gate(r, following, u)
                        up_value(r, following, u)
                y_T(c)

            def y_T(c):
                pe.wait_ge(yT_copied, c + 1)
                for t in range(TB):
                    i = nc.tensor.transpose(psY[:, N + t * P:N + (t + 1) * P], yT[:, t * P:(t + 1) * P], idn[:, :])
                i.then_inc(y_full, 1)

            def value_mm(b):
                pe.wait_ge(xT_lo_done[1], b + 1)
                for t in range(TB):
                    s = slice(t * P, (t + 1) * P)
                    i = mm3(psM[:, N + t * P:N + (t + 1) * P], xT_hi[1][:, s], xT_lo[1][:, s],
                            wsm_hi[:, CV:CV + P], wsm_lo[:, CV:CV + P])
                i.then_inc(v_psum, 1)

            def qk(b):
                pe.wait_ge(xT_lo_done[1], b + 1)
                for s in range(2):
                    c = slice(CQ + s * P, CQ + (s + 1) * P)
                    i = mm3(psM[:, s * N:(s + 1) * N], wsm_hi[:, c], wsm_lo[:, c], xT_hi[1][:, :], xT_lo[1][:, :])
                i.then_inc(qk_full, 1)

            def scores_1(b, i):
                qt, hp = i // 8, i % 8
                if i == 0:
                    pe.wait_ge(stack_landed, b * (16 * 2 * len(PAIRS)) + 16 * 2 * len(PAIRS))
                    if not (isinstance(b, int) and b == 0):
                        pe.wait_ge(exp_done, b * 16)
                if i >= 2:
                    pe.wait_ge(max_found, b * 32 + 2 * (i - 1))
                for j in range(2):
                    h = 2 * hp + j
                    m = nc.tensor.matmul(psS[i % 2][:, j * N:(j + 1) * N], qs[0:S_ROWS, h, qt * P:(qt + 1) * P],
                                         ks[0:S_ROWS, h, :], start=True, stop=True)
                m.then_inc(s1_full, 1)

            def max_T(b):
                pe.wait_ge(nm_done, b + 1)
                if isinstance(b, int) and b == 0:
                    pe.wait_ge(route[0], 2 * ROUTE + 4)
                else:
                    pe.wait_ge(route[1], (b - 1) * ROUTE + 4)
                for t in range(TB):
                    i = nc.tensor.transpose(psM[0:H, t * P:(t + 1) * P], nm[:, t, :], idn[:, :])
                i.then_inc(mT_full, 1)

            def scores_2(b, j, ln0=None):
                hp, kt = j // 2, j % 2
                if j == 0:
                    pe.wait_ge(mrow_landed, b * 16 + 16)
                    pe.wait_ge(max_found, b * 32 + 32)
                if j == 2 and ln0:
                    pe.wait_ge(route[0], (b + 2) * ROUTE + 4)
                if j == 2 and ln0 is False:
                    pe.wait_ge(sin_done, b * 2 + 4)
                if j >= 3:
                    pe.wait_ge(exp_done, b * 16 + (j - 2))
                for a in range(2):
                    h = 2 * hp + a
                    m = nc.tensor.matmul(score_banks[j % 3][:, a * N:(a + 1) * N], ks[0:E_ROWS, h, kt * P:(kt + 1) * P],
                                         qs[0:E_ROWS, h, :], start=True, stop=True)
                m.then_inc(s2_full, 1)

            def weighted_values(b, half):
                pe.wait_ge(exp_done, b * 16 + 8 * (half + 1))
                if half:
                    pe.wait_ge(att_done, b * 4 + 2)
                for a in range(2):
                    for kt in range(TB):
                        for j in range(4):
                            h = half * 8 + a * 4 + j
                            m = nc.tensor.matmul(psM[j * VW:(j + 1) * VW, a * N:(a + 1) * N], vaug[:, kt, h, :],
                                                 probs[:, kt, h, :], start=(kt == 0), stop=(kt == TB - 1),
                                                 tile_position=(0, j * VW))
                m.then_inc(pv_full, 1)

            def out_T(b, half):
                pe.wait_ge(oT_copied, b * 2 + (half + 1))
                for x4 in range(4):
                    m = nc.tensor.transpose(psM[:, x4 * P:(x4 + 1) * P], oT[:, x4 * P:(x4 + 1) * P], idn[:, :])
                m.then_inc(o_full, 1)

            def att_T(b):
                pe.wait_ge(att_done, b * 4 + 4)
                for t in range(TB):
                    m = nc.tensor.transpose(psM[:, t * P:(t + 1) * P], att[:, t, :], idn[:, :])
                m.then_inc(aT_full, 1)

            def project(b):
                pe.wait_ge(aT_lo_done, b + 1)
                for t in range(TB):
                    s, o = slice(t * P, (t + 1) * P), psM[:, t * P:(t + 1) * P]
                    mm3(o, aT_hi[:, s], aT_lo[:, s], wsm_hi[:, CP:CP + P], wsm_lo[:, CP:CP + P], stop=False)
                    m = nc.tensor.matmul(o, one_row[:, :], pb_row[:, :], start=False, stop=True)
                m.then_inc(proj_full, 1)

            def prologue():
                pe.wait_ge(idn_landed, 32)
                ln_T(0, 0)
                pe.wait_ge(wsm_lo_done, 1)
                logits(0, 0)
                for u in range(UNITS):
                    if u % TB == 0:
                        pe.wait_ge(wup_lo_done, u // TB + 1)
                    up_gate(0, 0, u)
                    up_value(0, 0, u)
                for ch in range(CH):
                    down_T(0, ch)
                    if ch == 8:
                        pe.wait_ge(gate_done[0], 1)
                        ln_T(0, 1)
                    if ch == 11:
                        logits(0, 1)
                    if ch >= LAG:
                        if ch - LAG in DOWN_STARTS:
                            pe.wait_ge(wdn_lo_done, DOWN_STARTS.index(ch - LAG) + 1)
                        down_mm(0, ch - LAG)
                down_end(0)
                for u in range(UNITS):
                    up_gate(0, 1, u)
                    if u == 4:
                        pe.wait_ge(route[0], ROUTE + 4)
                        ln_T(1, 0)
                    if u == 6:
                        value_mm(0)
                    if u == 7:
                        pe.wait_ge(v_copied, 1)
                        qk(0)
                    up_value(0, 1, u)
                for ch in range(CH):
                    down_T(1, ch)
                    if ch == 3:
                        pe.wait_ge(sin_done, 2)
                        ln_T(0, 2)
                    if ch == 6:
                        logits(0, 2)
                    if ch == 8:
                        pe.wait_ge(rows_landed, 64)
                        pe.wait_ge(const_landed, 32)
                    if ch >= S1_AT:
                        scores_1(0, ch - S1_AT)
                    if ch >= LAG:
                        down_mm(1, ch - LAG)
                down_end(1)
                for i in range(CH - S1_AT, 16):
                    scores_1(0, i)
                max_T(0)
                for j in range(16):
                    scores_2(0, j)
                for u in range(UP_FIRST):
                    up_gate(0, 2, u)
                    up_value(0, 2, u)

            def iteration(g, ln0):
                c1, c2 = call_1(g), call_2(g)
                for u in range(UNITS):
                    if u >= UP_FIRST:
                        up_gate(0, c1, u)
                    if u == AT["T1"]:
                        pe.wait_ge(exp_done, g * 16 + 16)
                        ln_T(1, g + 1)
                    if u == AT["qk"]:
                        qk(g + 1)
                    if u == AT["pv_0"]:
                        pe.wait_ge(sin_done, g * 2 + 4)
                        weighted_values(g, 0)
                    if u == AT["oT_0"]:
                        out_T(g, 0)
                    if u == AT["pv_1"]:
                        weighted_values(g, 1)
                    if u == AT["oT_1"]:
                        out_T(g, 1)
                    if u == AT["v"]:
                        pe.wait_ge(att_done, g * 4 + 4)
                        value_mm(g + 1)
                    if u >= UP_FIRST:
                        up_value(0, c1, u)
                for ch in range(CH):
                    down_T(c1, ch)
                    if ch == AT["aT"]:
                        pe.wait_ge(v_copied, g + 2)
                        att_T(g)
                    if ch == AT["project"]:
                        project(g)
                    if ch == AT["T2"]:
                        pe.wait_ge(x2_done, g + 1)
                        ln_T(2, g)
                    if ch == AT["logits_1"]:
                        logits(1, g)
                    if ch in PASS_1:
                        scores_1(g + 1, PASS_1[ch])
                    if ch >= LAG:
                        down_mm(c1, ch - LAG)
                down_end(c1, 1, c2)
                for u in range(UNITS):
                    if u >= UP_FIRST:
                        up_gate(1, c2, u)
                    if u in PASS_1_UP:
                        scores_1(g + 1, PASS_1_UP[u])
                    if u == AT["max_T"]:
                        max_T(g + 1)
                    if u == AT["T0"]:
                        pe.wait_ge(ml_done, g + 2)
                        if ln0:
                            ln_T(0, g + 3)
                        else:
                            ln_T(1, g + 2)
                    if not ln0 and u == AT["T0"] + 2:
                        qk(g + 2)
                    if ln0 and u == AT["logits_0"]:
                        logits(0, g + 3)
                    if u >= UP_FIRST:
                        up_value(1, c2, u)
                for ch in range(CH):
                    down_T(c2, ch)
                    if ch in PASS_2:
                        scores_2(g + 1, PASS_2[ch], ln0)
                    if ch >= LAG:
                        down_mm(c2, ch - LAG)
                down_end(c2, 0, call_1(g + 1) if ln0 else None)

            def ending():
                pe.wait_ge(exp_done, PENULT * 16 + 16)
                weighted_values(PENULT, 0)
                out_T(PENULT, 0)
                weighted_values(PENULT, 1)
                for i in range(16):
                    scores_1(LAST, i)
                    if i == 1:
                        out_T(PENULT, 1)
                    if i == 3:
                        pe.wait_ge(att_done, PENULT * 4 + 4)
                        value_mm(LAST)
                    if i == 5:
                        pe.wait_ge(v_copied, LAST + 1)
                        att_T(PENULT)
                    if i == 7:
                        project(PENULT)
                    if i == 11:
                        pe.wait_ge(x2_done, PENULT + 1)
                        ln_T(2, PENULT)
                    if i == 13:
                        logits(1, PENULT)
                for u in range(UNITS):
                    up_gate(1, CALL_P, u)
                    if u == 3:
                        max_T(LAST)
                    up_value(1, CALL_P, u)
                for ch in range(CH):
                    down_T(CALL_P, ch)
                    if ch in PASS_2_END:
                        scores_2(LAST, PASS_2_END[ch])
                    if ch == 17:
                        pe.wait_ge(exp_done, LAST * 16 + 16)
                        weighted_values(LAST, 0)
                    if ch == 19:
                        out_T(LAST, 0)
                    if ch == 21:
                        weighted_values(LAST, 1)
                    if ch >= LAG:
                        down_mm(CALL_P, ch - LAG)
                down_end(CALL_P)
                out_T(LAST, 1)
                att_T(LAST)
                project(LAST)
                pe.wait_ge(x2_done, LAST + 1)
                ln_T(2, LAST)
                logits(1, LAST)
                for u in range(UNITS):
                    up_gate(1, CALL_L, u)
                    up_value(1, CALL_L, u)
                for ch in range(CH):
                    down_T(CALL_L, ch)
                    if ch >= LAG:
                        down_mm(CALL_L, ch - LAG)
                down_end(CALL_L)

            iterations(pe, prologue, iteration, ending)


def _constants():
    import numpy as np

    ident = np.eye(P, dtype=np.float32)
    pos = np.arange(N)
    dist = np.minimum(pos[None, :P] - pos[:P, None], 0).astype(np.float32)
    inv = (np.float32(1.0) / np.float32(10000.0) ** (np.arange(0, HD, 2, dtype=np.float32) / np.float32(HD))).astype(np.float32)
    angle = (pos.astype(np.float32)[None, :] * inv[:, None]).astype(np.float64)
    d = np.arange(HD)
    cos = np.cos(angle)[d % (HD // 2)]
    sin = np.sin(angle)[d % (HD // 2)] * np.where(d < HD // 2, 1.0, -1.0)[:, None]
    rope = np.stack([cos, sin], 1)[:, None] * HD ** -0.25
    rope = np.broadcast_to(rope, (HD, H, 2, N)).reshape(P, 2, N).astype(np.float32)
    ids = np.broadcast_to(np.arange(E, dtype=np.float32), (P, TB, E))
    key, query = np.where(pos < P, pos - (P - 1), 0), np.where(pos >= P, (P - 1) - pos, 0)
    far = np.broadcast_to(np.stack([key, query]).astype(np.float32), (H, 2, N))
    rows = np.stack([pos >= P] * 3 + [pos < P] * 3 + [pos >= 0] * 2).astype(np.dtype("bfloat16"))
    rows = np.broadcast_to(rows[:, None, :], (8, H, N))
    return [np.ascontiguousarray(a) for a in (ident, dist, dist.T, rope, ids, far, rows)]


def kernel(L0_attn_x, L0_attn_qkv_w, L0_attn_proj_w, L0_attn_proj_b, L0_attn_slopes, L0_ffn_router_w, L0_ffn_w1,
           L0_ffn_v1, L0_ffn_w2, L0_ffn_bias):
    import concourse.bacc as bacc
    import numpy as np
    from concourse.bass_utils import run_bass_kernel_spmd

    qkv = np.asarray(L0_attn_qkv_w).reshape(3, H, HD, D)
    q, k = qkv[0].transpose(1, 0, 2), qkv[1].transpose(1, 0, 2)
    small = [b.reshape(P, D).T for b in (q, k)] + [qkv[2].reshape(P, D).T, np.asarray(L0_attn_proj_w).T,
                                                   np.asarray(L0_ffn_router_w)]
    ident, dist, dist_t, rope, ids, far, rows = _constants()
    arrays = {
        "x": L0_attn_x, "small_w": np.concatenate(small, 1), "w1": L0_ffn_w1, "v1": L0_ffn_v1, "w2": L0_ffn_w2,
        "ffn_bias": L0_ffn_bias, "proj_b": L0_attn_proj_b, "slopes": L0_attn_slopes, "ident": ident, "dist": dist,
        "dist_t": dist_t, "rope": rope, "expert_ids": ids, "far": far, "ones_rows": rows,
    }
    arrays = {"in_" + n: np.ascontiguousarray(a) for n, a in arrays.items()}
    nc = bacc.Bacc("TRN2", target_bir_lowering=False, num_devices=1)
    args = [nc.dram_tensor(n, a.shape, mybir.dt.from_np(a.dtype), kind="ExternalInput").ap() for n, a in arrays.items()]
    out = nc.dram_tensor("out", (B, N, D), F32, kind="ExternalOutput").ap()
    macaron(nc, *args, out)
    return run_bass_kernel_spmd(nc, [arrays], core_ids=[0]).results[0]["out"]
```
